# Optimizing a Trainium2 kernel written in Bass

```python
import numpy as np
import jax
import jax.numpy as jnp

def _softmax(x, axis=-1):
    return jax.nn.softmax(x, axis=axis)

def _gelu(x):
    return jax.nn.gelu(x, approximate=True)

def _silu(x):
    return jax.nn.silu(x)

def _sigmoid(x):
    return jax.nn.sigmoid(x)

def _layernorm(x, axis=-1, eps=1e-05):
    m = jnp.mean(x, axis=axis, keepdims=True)
    v = jnp.var(x, axis=axis, keepdims=True)
    return (x - m) / jnp.sqrt(v + eps)

def _scatter_add(tgt, idx, src, axis=0):
    return tgt.at[idx].add(src)

def _segment_sum(src, seg, n):
    return jax.ops.segment_sum(src, seg, n)
kernel_name = 'mk_macaron_d1_jaxref_r8_4f4652'

def setup_inputs(seed: int=0):
    np.random.seed(seed)
    _w = jnp.asarray

    def _L0_attn_setup():
        import jax, jax.numpy as jnp
        import numpy as np
        B, T, C, H = (2, 256, 256, 16)
        D = C // H
        EPS = 1e-05

        def _wkv_scan(r, k, v, w, u):
            rT = jnp.moveaxis(r, 1, 0)
            kT = jnp.moveaxis(k, 1, 0)
            vT = jnp.moveaxis(v, 1, 0)

            def step(S, inp):
                r_t, k_t, v_t = inp
                kv = k_t[..., :, None] * v_t[..., None, :]
                o = jnp.einsum('bhi,bhij->bhj', r_t, S + u[None, :, :, None] * kv)
                S = w[None, :, :, None] * S + kv
                return (S, o)
            S0 = jnp.zeros((r.shape[0], H, D, D), r.dtype)
            _, o = jax.lax.scan(step, S0, (rT, kT, vT))
            return jnp.moveaxis(o, 0, 1)
        key = jax.random.key(seed)
        ks = jax.random.split(key, 12)
        return {'x': jax.random.normal(ks[0], (B, T, C), jnp.float32), 'Wr': jax.random.normal(ks[1], (C, C), jnp.float32) * (1.0 / np.sqrt(C)), 'Wk': jax.random.normal(ks[2], (C, C), jnp.float32) * (1.0 / np.sqrt(C)), 'Wv': jax.random.normal(ks[3], (C, C), jnp.float32) * (1.0 / np.sqrt(C)), 'Wg': jax.random.normal(ks[4], (C, C), jnp.float32) * (1.0 / np.sqrt(C)), 'Wo': jax.random.normal(ks[5], (C, C), jnp.float32) * (1.0 / np.sqrt(C)), 'time_decay': jax.random.normal(ks[6], (H, D), jnp.float32), 'time_first': jax.random.normal(ks[7], (H, D), jnp.float32) * 0.1, 'tm_k': jax.random.uniform(ks[8], (C,), jnp.float32, -0.1, 0.1) + 1.0, 'tm_v': jax.random.uniform(ks[9], (C,), jnp.float32, -0.1, 0.1) + 1.0, 'tm_r': jax.random.uniform(ks[10], (C,), jnp.float32, -0.1, 0.1) + 1.0, 'tm_g': jax.random.uniform(ks[11], (C,), jnp.float32, -0.1, 0.1) + 1.0, 'ln_w': jnp.ones((C,), jnp.float32), 'ln_b': jnp.zeros((C,), jnp.float32)}
    _L0_attn_in = _L0_attn_setup()

    def _L0_ffn_setup():
        import jax, jax.numpy as jnp
        import numpy as np
        H = 256
        I = 176
        E = 16
        G = 4
        TOPK_GROUP = 2
        TOP_K = 6
        N_SHARED = 2
        SCALE_FACTOR = 2.5
        B, S = (2, 256)

        def _gate(hs_flat, gate_weight, bias):
            T = hs_flat.shape[0]
            logits = hs_flat @ gate_weight.T
            scores = jax.nn.sigmoid(logits)
            scores_for_choice = scores + bias[None, :]
            gs = scores_for_choice.reshape(T, G, E // G)
            group_scores = jnp.sum(jax.lax.top_k(gs, 2)[0], axis=-1)
            _, group_idx = jax.lax.top_k(group_scores, TOPK_GROUP)
            group_mask = jnp.zeros((T, G), scores.dtype).at[jnp.arange(T)[:, None], group_idx].set(1.0)
            score_mask = jnp.repeat(group_mask, E // G, axis=1)
            tmp_scores = jnp.where(score_mask > 0, scores_for_choice, 0.0)
            _, topk_idx = jax.lax.top_k(tmp_scores, TOP_K)
            topk_weight = jnp.take_along_axis(scores, topk_idx, axis=1)
            topk_weight = topk_weight / (jnp.sum(topk_weight, axis=-1, keepdims=True) + 1e-20)
            topk_weight = topk_weight * SCALE_FACTOR
            return (topk_idx, topk_weight)
        key = jax.random.key(seed)
        ks = jax.random.split(key, 8)
        scale = 0.01
        SI = I * N_SHARED
        return {'hidden_states': jax.random.normal(ks[0], (B, S, H), jnp.float32), 'gate_weight': jax.random.uniform(ks[1], (E, H), jnp.float32, -0.05, 0.05), 'e_score_correction_bias': jnp.zeros((E,), jnp.float32), 'gate_proj': jax.random.normal(ks[2], (E, I, H), jnp.float32) * scale, 'up_proj': jax.random.normal(ks[3], (E, I, H), jnp.float32) * scale, 'down_proj': jax.random.normal(ks[4], (E, H, I), jnp.float32) * scale, 'shared_gate_w': jax.random.normal(ks[5], (SI, H), jnp.float32) * scale, 'shared_up_w': jax.random.normal(ks[6], (SI, H), jnp.float32) * scale, 'shared_down_w': jax.random.normal(ks[7], (H, SI), jnp.float32) * scale}
    _L0_ffn_in = _L0_ffn_setup()
    _d = {'L0_attn_x': _L0_attn_in['x'], 'L0_attn_Wr': _L0_attn_in['Wr'], 'L0_attn_Wk': _L0_attn_in['Wk'], 'L0_attn_Wv': _L0_attn_in['Wv'], 'L0_attn_Wg': _L0_attn_in['Wg'], 'L0_attn_Wo': _L0_attn_in['Wo'], 'L0_attn_time_decay': _L0_attn_in['time_decay'], 'L0_attn_time_first': _L0_attn_in['time_first'], 'L0_attn_tm_k': _L0_attn_in['tm_k'], 'L0_attn_tm_v': _L0_attn_in['tm_v'], 'L0_attn_tm_r': _L0_attn_in['tm_r'], 'L0_attn_tm_g': _L0_attn_in['tm_g'], 'L0_attn_ln_w': _L0_attn_in['ln_w'], 'L0_attn_ln_b': _L0_attn_in['ln_b'], 'L0_ffn_gate_weight': _L0_ffn_in['gate_weight'], 'L0_ffn_e_score_correction_bias': _L0_ffn_in['e_score_correction_bias'], 'L0_ffn_gate_proj': _L0_ffn_in['gate_proj'], 'L0_ffn_up_proj': _L0_ffn_in['up_proj'], 'L0_ffn_down_proj': _L0_ffn_in['down_proj'], 'L0_ffn_shared_gate_w': _L0_ffn_in['shared_gate_w'], 'L0_ffn_shared_up_w': _L0_ffn_in['shared_up_w'], 'L0_ffn_shared_down_w': _L0_ffn_in['shared_down_w']}
    _x0 = _d['L0_attn_x']
    _d['L0_attn_x'] = jax.random.normal(jax.random.fold_in(jax.random.key(seed), 1), (4, 256, 256), dtype=_x0.dtype)
    del _x0
    return _d

def reference(L0_attn_x, L0_attn_Wr, L0_attn_Wk, L0_attn_Wv, L0_attn_Wg, L0_attn_Wo, L0_attn_time_decay, L0_attn_time_first, L0_attn_tm_k, L0_attn_tm_v, L0_attn_tm_r, L0_attn_tm_g, L0_attn_ln_w, L0_attn_ln_b, L0_ffn_gate_weight, L0_ffn_e_score_correction_bias, L0_ffn_gate_proj, L0_ffn_up_proj, L0_ffn_down_proj, L0_ffn_shared_gate_w, L0_ffn_shared_up_w, L0_ffn_shared_down_w):

    def _L0_attn_ref(x, Wr, Wk, Wv, Wg, Wo, time_decay, time_first, tm_k, tm_v, tm_r, tm_g, ln_w, ln_b):
        import jax, jax.numpy as jnp
        import numpy as np
        B, T, C, H = (2, 256, 256, 16)
        D = C // H
        EPS = 1e-05

        def _wkv_scan(r, k, v, w, u):
            rT = jnp.moveaxis(r, 1, 0)
            kT = jnp.moveaxis(k, 1, 0)
            vT = jnp.moveaxis(v, 1, 0)

            def step(S, inp):
                r_t, k_t, v_t = inp
                kv = k_t[..., :, None] * v_t[..., None, :]
                o = jnp.einsum('bhi,bhij->bhj', r_t, S + u[None, :, :, None] * kv)
                S = w[None, :, :, None] * S + kv
                return (S, o)
            S0 = jnp.zeros((r.shape[0], H, D, D), r.dtype)
            _, o = jax.lax.scan(step, S0, (rT, kT, vT))
            return jnp.moveaxis(o, 0, 1)
        Bx, Tx, Cx = x.shape
        xx = jnp.concatenate([x[:, 1:2, :], x[:, :-1, :]], axis=1) - x
        xk = x + xx * tm_k
        xv = x + xx * tm_v
        xr = x + xx * tm_r
        xg = x + xx * tm_g
        r = xr @ Wr.T
        k = xk @ Wk.T
        v = xv @ Wv.T
        g = jax.nn.sigmoid(xg @ Wg.T)
        w = jnp.exp(-jnp.exp(time_decay))
        r = r.reshape(Bx, Tx, H, D)
        k = k.reshape(Bx, Tx, H, D)
        v = v.reshape(Bx, Tx, H, D)
        o = _wkv_scan(r, k, v, w, time_first)
        o = o.reshape(Bx, Tx, Cx)
        y = o * g @ Wo.T
        mu = jnp.mean(y, axis=-1, keepdims=True)
        var = jnp.mean((y - mu) ** 2, axis=-1, keepdims=True)
        return (y - mu) * jax.lax.rsqrt(var + EPS) * ln_w + ln_b

    def _L0_ffn_ref(hidden_states, gate_weight, e_score_correction_bias, gate_proj, up_proj, down_proj, shared_gate_w, shared_up_w, shared_down_w):
        import jax, jax.numpy as jnp
        import numpy as np
        H = 256
        I = 176
        E = 16
        G = 4
        TOPK_GROUP = 2
        TOP_K = 6
        N_SHARED = 2
        SCALE_FACTOR = 2.5
        B, S = (2, 256)

        def _gate(hs_flat, gate_weight, bias):
            T = hs_flat.shape[0]
            logits = hs_flat @ gate_weight.T
            scores = jax.nn.sigmoid(logits)
            scores_for_choice = scores + bias[None, :]
            gs = scores_for_choice.reshape(T, G, E // G)
            group_scores = jnp.sum(jax.lax.top_k(gs, 2)[0], axis=-1)
            _, group_idx = jax.lax.top_k(group_scores, TOPK_GROUP)
            group_mask = jnp.zeros((T, G), scores.dtype).at[jnp.arange(T)[:, None], group_idx].set(1.0)
            score_mask = jnp.repeat(group_mask, E // G, axis=1)
            tmp_scores = jnp.where(score_mask > 0, scores_for_choice, 0.0)
            _, topk_idx = jax.lax.top_k(tmp_scores, TOP_K)
            topk_weight = jnp.take_along_axis(scores, topk_idx, axis=1)
            topk_weight = topk_weight / (jnp.sum(topk_weight, axis=-1, keepdims=True) + 1e-20)
            topk_weight = topk_weight * SCALE_FACTOR
            return (topk_idx, topk_weight)
        b, s, h = hidden_states.shape
        hs = hidden_states.reshape(-1, h)
        T = hs.shape[0]
        topk_idx, topk_weight = _gate(hs, gate_weight, e_score_correction_bias)
        comb = jnp.zeros((T, E), hs.dtype).at[jnp.arange(T)[:, None], topk_idx].add(topk_weight)
        out = jnp.zeros_like(hs)
        for e in range(E):
            g = hs @ gate_proj[e].T
            u = hs @ up_proj[e].T
            inter = jax.nn.silu(g) * u
            out = out + comb[:, e:e + 1] * (inter @ down_proj[e].T)
        y = out.reshape(b, s, h)
        sg = hidden_states @ shared_gate_w.T
        su = hidden_states @ shared_up_w.T
        shared_out = jax.nn.silu(sg) * su @ shared_down_w.T
        return y + shared_out
    x = L0_attn_x
    x = x + 0.5 * _L0_ffn_ref(_layernorm(x, axis=-1), L0_ffn_gate_weight, L0_ffn_e_score_correction_bias, L0_ffn_gate_proj, L0_ffn_up_proj, L0_ffn_down_proj, L0_ffn_shared_gate_w, L0_ffn_shared_up_w, L0_ffn_shared_down_w)
    x = x + _L0_attn_ref(_layernorm(x, axis=-1), L0_attn_Wr, L0_attn_Wk, L0_attn_Wv, L0_attn_Wg, L0_attn_Wo, L0_attn_time_decay, L0_attn_time_first, L0_attn_tm_k, L0_attn_tm_v, L0_attn_tm_r, L0_attn_tm_g, L0_attn_ln_w, L0_attn_ln_b)
    x = x + 0.5 * _L0_ffn_ref(_layernorm(x, axis=-1), L0_ffn_gate_weight, L0_ffn_e_score_correction_bias, L0_ffn_gate_proj, L0_ffn_up_proj, L0_ffn_down_proj, L0_ffn_shared_gate_w, L0_ffn_shared_up_w, L0_ffn_shared_down_w)
    return x

_drawn_inputs = setup_inputs


def setup_inputs(seed=0):
    import zlib

    import numpy as np

    out = dict(_drawn_inputs(seed))
    spreads = {'L0_attn_ln_w': (1.0, 0.2),
     'L0_attn_ln_b': (0.0, 0.1),
     'L0_ffn_e_score_correction_bias': (0.0, 0.8)}
    factors = {'L0_ffn_gate_weight': 8.0,
     'L0_ffn_gate_proj': 8.0,
     'L0_ffn_up_proj': 8.0,
     'L0_ffn_down_proj': 8.0,
     'L0_ffn_shared_gate_w': 8.0,
     'L0_ffn_shared_up_w': 8.0,
     'L0_ffn_shared_down_w': 8.0}
    for name, (base, spread) in spreads.items():
        noise = np.random.default_rng([zlib.crc32(name.encode()), seed]).standard_normal(out[name].shape)
        drawn = base * np.exp(spread * noise) if base else spread * noise
        out[name] = jnp.asarray(drawn.astype(out[name].dtype))
    for name, factor in factors.items():
        out[name] = (out[name] * factor).astype(out[name].dtype)
    return out
```

```python
from contextlib import ExitStack

import concourse.bass as bass
import numpy as np
from concourse import mybir

F32 = mybir.dt.float32
F32R = mybir.dt.float32r
ALU = mybir.AluOpType
ACT = mybir.ActivationFunctionType
AX_X = mybir.AxisListType.X

P = 128
BATCH, SEQ, C = 4, 256, 256
TOKENS = BATCH * SEQ
HALVES = 2
N = TOKENS // HALVES
HB = BATCH // HALVES
K = C // P
HEADS, D = 16, 16
E, I, GROUPS, TOP_GROUPS, TOP_K, N_SHARED = 16, 176, 4, 2, 6, 2
ROUTE_SCALE = 2.5
EPS = 1e-5
SHARED_TILES = -(-I * N_SHARED // P)
EXPERT_TILES = E * I // P
TILES = SHARED_TILES + EXPERT_TILES
PASSES = 2 * HALVES
STEPS = PASSES * TILES
WCOLS = 2 * K * P + C
TT = N // P
UNITS = K * D

RAW, WR, BR, PR = 3, 3, 2, 3

C_ONES, C_HEAD, C_IDENT, C_RED = 0, P, 2 * P, 3 * P
C_GATE = C_RED + D * P
C_BIAS = C_GATE + K * E
C_RSTE = C_BIAS + E
C_RSTG = C_RSTE + TT * E
C_PAR = C_RSTG + TT * GROUPS
PARAMS = ("time_decay", "time_first", "tm_v", "tm_k", "tm_r", "tm_g", "ln_w", "ln_b")
C_END = C_PAR + K * len(PARAMS)
MIX = ("v", "k", "r", "g")

AT_SPLIT = 6
AT_LN_NEXT, AT_ROUTE_NEXT = 12, 13
AT_ATT_LN, AT_PROJ = 1, 2
AT_UNITS, UNITS_PER_STEP = 6, 3
AT_POST = AT_UNITS + -(-(UNITS + 2) // UNITS_PER_STEP)
AT_OUT_LN = AT_POST + 1
AT_FFN_LN = AT_OUT_LN + 1
AT_ROUTE = AT_FFN_LN + 1
assert AT_ROUTE < TILES

NORM = {"f0": 0, "f1": 1, "a0": 2, "o0": 3, "f2": 4, "a1": 5, "o1": 6, "f3": 7}


def macaron(nc, x_d, w_d, aw_d, c_d, sel_d, exp_d, out_d):
    ctx = ExitStack()
    with ctx:
        def sb(name, shape, dt=F32):
            return ctx.enter_context(nc.sbuf_tensor(name, shape, dt))

        def pb(name, shape):
            return ctx.enter_context(nc.psum_tensor(name, shape, F32))

        def sem(name):
            return ctx.enter_context(nc.semaphore(name))

        cst = sb("cst", [P, C_END])
        sel_j = sb("sel_j", [P, D, P], F32R)
        sel_e = sb("sel_e", [2 * E, EXPERT_TILES, P], F32R)
        ones_c = cst[:, C_ONES:C_ONES + P]
        head_ones = cst[:, C_HEAD:C_HEAD + P]
        ident = cst[:, C_IDENT:C_IDENT + P]
        gate_t = cst[:, C_GATE:C_GATE + K * E].rearrange("p (k e) -> p k e", k=K)
        bias = cst[:, C_BIAS:C_BIAS + E]

        def red_j(j):
            return cst[:, C_RED + j * P:C_RED + (j + 1) * P]

        def par(name, k):
            at = C_PAR + K * PARAMS.index(name) + k
            return cst[:, at:at + 1]

        eps = sb("eps", [P, 1])
        lam = sb("lam", [P, K])
        decay = sb("decay", [P, K])
        decay_t = sb("decay_t", [P, K, N])
        early = sb("early", [P, (2 + PR) * N])
        assert (2 + PR) * N == 5 * K * C
        aw_raw = early[:].rearrange("p (m k c) -> p m k c", m=5, k=K)
        aw_hi = sb("aw_hi", [P, 5, K, C], F32R)
        aw_lo = sb("aw_lo", [P, 5, K, C], F32R)
        x = sb("x", [P, K, TOKENS])
        w_raw = sb("w_raw", [P, RAW, WCOLS])
        w_hi = sb("w_hi", [P, WR, WCOLS], F32R)
        w_lo = sb("w_lo", [P, WR, WCOLS], F32R)
        hf = sb("hf", [P, K, N])
        h_hi = sb("h_hi", [P, 2, K, N], F32R)
        h_lo = sb("h_lo", [P, 2, K, N], F32R)
        sil = sb("sil", [P, BR, N])
        inter = sb("inter", [P, BR, N])
        in_hi = sb("in_hi", [P, BR, N], F32R)
        in_lo = sb("in_lo", [P, BR, N], F32R)
        xc = sb("xc", [P, K, N])
        sq = sb("sq", [P, K, N])
        sd = sb("sd", [P, N])
        rstd = sb("rstd", [P, N])
        score = sb("score", [P, TT, E])
        choice = sb("choice", [P, TT, E])
        pair = sb("pair", [P, 2, TT * GROUPS, 2])
        g4 = sb("g4", [P, 8, TT, GROUPS])
        g1 = sb("g1", [P, 8, TT])
        rt = sb("rt", [P, 5, TT, E])
        top8 = sb("top8", [P, TT, 8])
        comb2 = sb("comb2", [P, TT, 2, E], F32R)
        comb_t = sb("comb_t", [2 * E, 2, N], F32R)
        ha = sb("ha", [P, K, N])
        xx = sb("xx", [P, K, N])
        xm = sb("xm", [P, 2, K, N])
        xm_hi = sb("xm_hi", [P, 2, K, N], F32R)
        xm_lo = sb("xm_lo", [P, 2, K, N], F32R)
        proj = {m: sb(f"{m}_t", [P, K, N]) for m in MIX}
        v_hi, v_lo = xm_hi[:, 0], xm_lo[:, 0]
        kv = early[:, 0:2 * N].rearrange("p (r t) -> p r t", r=2)
        state = sb("state", [P, 2, N + 1])
        rs = early[:, 2 * N:].rearrange("p (r t) -> p r t", r=PR)
        og, og_hi, og_lo = xm[:, 1], xm_hi[:, 1], xm_lo[:, 1]
        ysb = xm[:, 0]

        Y = pb("Y", [P, K, N])
        G = pb("G", [P, N])
        U = pb("U", [P, N])
        CB = pb("CB", [P, N])
        O = pb("O", [P, N])
        A = [pb("A0", [P, N]), pb("A1", [P, N])]

        c_loaded, aw_loaded, sel_loaded = sem("c_loaded"), sem("aw_loaded"), sem("sel_loaded")
        x_loaded = [sem(f"x_loaded{half}") for half in range(HALVES)]
        w_loaded = [sem(f"w_loaded{i}") for i in range(RAW)]
        eps_set, lam_done, decay_done, dt_set, dt_done = (
            sem("eps_set"), sem("lam_done"), sem("decay_done"), sem("dt_set"), sem("dt_done"))
        state0_set = sem("state0_set")
        aw_hi_done, aw_lo_done = sem("aw_hi_done"), sem("aw_lo_done")
        ln_mean, ln_xc, ln_sq, ln_var, ln_sd, ln_rstd, ln_h = (
            sem(n) for n in ("ln_mean", "ln_xc", "ln_sq", "ln_var", "ln_sd", "ln_rstd", "ln_h"))
        h_hi_done, h_lo_done = sem("h_hi_done"), sem("h_lo_done")
        w_hi_done, w_lo_done = sem("w_hi_done"), sem("w_lo_done")
        g_done, u_done, cb_done, down_done = sem("g_done"), sem("u_done"), sem("cb_done"), sem("down_done")
        sil_done, up_done, scaled_done = sem("sil_done"), sem("up_done"), sem("scaled_done")
        in_hi_done, in_lo_done, ffn_added = sem("in_hi_done"), sem("in_lo_done"), sem("ffn_added")
        logits_done, tanh_done, route_step, comb_done, comb_tr, comb_t_done = (
            sem(n) for n in ("logits_done", "tanh_done", "route_step", "comb_done", "comb_tr", "comb_t_done"))
        xx_done, xm_done, xm_hi_done, xm_lo_done, proj_mm, proj_out = (
            sem(n) for n in ("xx_done", "xm_done", "xm_hi_done", "xm_lo_done", "proj_mm", "proj_out"))
        gate_sig, ruk_done, r_masked, v_hi_done, v_lo_done, diag_mm, diag_v = (
            sem(n) for n in ("gate_sig", "ruk_done", "r_masked", "v_hi_done", "v_lo_done", "diag_mm", "diag_v"))
        vb_done, kv_done, scan_done, rs_done, red_done, o_added, o_gated = (
            sem(n) for n in ("vb_done", "kv_done", "scan_done", "rs_done", "red_done", "o_added", "o_gated"))
        og_hi_done, og_lo_done, wo_mm, y_out, z_step, att_added = (
            sem(n) for n in ("og_hi_done", "og_lo_done", "wo_mm", "y_out", "z_step", "att_added"))
        out_stored = sem("out_stored")

        block = ctx.enter_context(nc.Block())

        def half_x(half):
            return x[:, :, half * N:(half + 1) * N]

        def over_k(ap):
            return ap.unsqueeze(1).broadcast_to([P, K, N])

        def experts_before(s):
            return s // TILES * EXPERT_TILES + max(0, s % TILES - SHARED_TILES)

        def is_expert(s):
            return s % TILES >= SHARED_TILES

        def units_of(p, t):
            if p not in (1, 2) or not AT_UNITS <= t < AT_POST:
                return range(0)
            first = (t - AT_UNITS) * UNITS_PER_STEP
            return range(first, min(first + UNITS_PER_STEP, UNITS + 2))

        @block.sync
        def _(sp):
            sp.dma_start(half_x(0), x_d[:, :, 0:N]).then_inc(x_loaded[0], 16)
            for s in range(STEPS):
                if s >= RAW:
                    sp.wait_ge(w_lo_done, s - RAW + 1)
                sp.dma_start(w_raw[:, s % RAW, :], w_d[s % TILES]).then_inc(w_loaded[s % RAW], 16)
                if s == 1:
                    sp.dma_start(half_x(1), x_d[:, :, N:TOKENS]).then_inc(x_loaded[1], 16)
                if s == 2:
                    sp.dma_start(aw_raw, aw_d).then_inc(aw_loaded, 16)
            for half in range(HALVES):
                sp.wait_ge(ffn_added, HALVES + half + 1)
                sp.dma_start(out_d[:, :, half * N:(half + 1) * N], half_x(half)).then_inc(out_stored, 16)
            sp.wait_ge(out_stored, 16 * HALVES)

        @block.gpsimd
        def _(pool):
            pool.dma_start(sel_e[:], exp_d).then_inc(sel_loaded, 16)
            pool.dma_start(sel_j[:], sel_d).then_inc(sel_loaded, 16)
            nc.gpsimd.memset(eps[:], EPS).then_inc(eps_set, 1)
            nc.gpsimd.memset(state[:, :, 0:1], 0.0).then_inc(state0_set, 1)
            nc.gpsimd.memset(decay_t[:], 1.0).then_inc(dt_set, 1)
            pool.wait_ge(dt_set, 1)
            starts = decay_t[:].rearrange("p k (b t) -> p (k b) t", t=SEQ)[:, :, 0:1]
            nc.gpsimd.memset(starts, 0.0).then_inc(dt_set, 1)

            def split_w(s):
                pool.wait_ge(w_loaded[s % RAW], 16 * (s // RAW + 1))
                pool.wait_ge(w_hi_done, s + 1)
                if s >= WR:
                    pool.wait_ge(down_done, s - WR + 1)
                nc.gpsimd.tensor_tensor(w_lo[:, s % WR, :], w_raw[:, s % RAW, :],
                                        w_hi[:, s % WR, :].bitcast(F32), ALU.subtract).then_inc(w_lo_done, 1)

            split_w(0)
            for s in range(STEPS):
                if s + 1 < STEPS:
                    split_w(s + 1)
                pool.wait_ge(in_hi_done, s + 1)
                if s >= BR:
                    pool.wait_ge(down_done, s - BR + 1)
                nc.gpsimd.tensor_tensor(in_lo[:, s % BR, :], inter[:, s % BR, :],
                                        in_hi[:, s % BR, :].bitcast(F32), ALU.subtract).then_inc(in_lo_done, 1)

        @block.scalar
        def _(act):
            act.dma_start(cst[:], c_d).then_inc(c_loaded, 16)
            act.wait_ge(c_loaded, 16)
            td = cst[:, C_PAR:C_PAR + K]
            nc.scalar.activation(lam[:], td, ACT.Exp).then_inc(lam_done, 1)
            act.wait_ge(lam_done, 1)
            nc.scalar.activation(decay[:], lam[:], ACT.Exp, scale=-1.0).then_inc(decay_done, 1)
            act.wait_ge(eps_set, 1)

            def norm(n):
                act.wait_ge(ln_xc, n + 1)
                if n:
                    act.wait_ge(ln_var, n)
                nc.scalar.activation(sq[:], xc[:], ACT.Square).then_inc(ln_sq, 1)
                act.wait_ge(ln_var, n + 1)
                if n:
                    act.wait_ge(ln_rstd, n)
                nc.scalar.activation(sd[:], A[1][:], ACT.Sqrt, bias=eps[:, 0:1]).then_inc(ln_sd, 1)

            def h_high(p):
                act.wait_ge(ln_h, NORM[f"f{p}"] + 1)
                if p >= 2:
                    act.wait_ge(u_done, (p - 1) * TILES)
                nc.scalar.copy(h_hi[:, p % 2], hf[:]).then_inc(h_hi_done, 1)

            def route(p):
                act.wait_ge(logits_done, p + 1)
                if p:
                    act.wait_ge(comb_done, p)
                nc.scalar.activation(score[:], A[0][:, 0:TT * E].rearrange("p (t e) -> p t e", t=TT),
                                     ACT.Tanh, scale=0.5).then_inc(tanh_done, 1)

            def route_out(p):
                act.wait_ge(comb_tr, p + 1)
                if p >= 2:
                    act.wait_ge(cb_done, (p - 1) * EXPERT_TILES)
                nc.scalar.copy(comb_t[:, p % 2], A[1][0:2 * E, :]).then_inc(comb_t_done, 1)

            def w_high(s):
                act.wait_ge(w_loaded[s % RAW], 16 * (s // RAW + 1))
                if s >= WR:
                    act.wait_ge(down_done, s - WR + 1)
                nc.scalar.copy(w_hi[:, s % WR, :], w_raw[:, s % RAW, :]).then_inc(w_hi_done, 1)

            def tile(s):
                act.wait_ge(g_done, s + 1)
                if s >= BR:
                    act.wait_ge(up_done, s - BR + 1)
                nc.scalar.activation(sil[:, s % BR, :], G[:], ACT.Silu).then_inc(sil_done, 1)

            def tile_high(s):
                if is_expert(s):
                    act.wait_ge(scaled_done, experts_before(s) + 1)
                else:
                    act.wait_ge(up_done, s + 1)
                if s >= BR:
                    act.wait_ge(down_done, s - BR + 1)
                nc.scalar.copy(in_hi[:, s % BR, :], inter[:, s % BR, :]).then_inc(in_hi_done, 1)

            def mix_high(a, m):
                i = len(MIX) * a + m
                act.wait_ge(xm_done, 2 * (i + 1))
                if i >= 2:
                    act.wait_ge(proj_mm, K * (i - 1))
                if m < 2 and a:
                    act.wait_ge(vb_done, UNITS * a)
                    act.wait_ge(wo_mm, K * a)
                nc.scalar.copy(xm_hi[:, m % 2], xm[:, m % 2]).then_inc(xm_hi_done, 1)

            def project_out(a, m):
                for k in range(K):
                    i = K * (len(MIX) * a + m) + k
                    act.wait_ge(proj_mm, i + 1)
                    if a:
                        act.wait_ge(o_gated, K)
                    func = ACT.Tanh if MIX[m] == "g" else ACT.Copy
                    nc.scalar.activation(proj[MIX[m]][:, k, :], A[k][:], func,
                                         scale=0.5 if MIX[m] == "g" else 1.0).then_inc(proj_out, 1)

            def v_high(a):
                act.wait_ge(proj_mm, K * len(MIX) * (a + 1))
                nc.scalar.copy(v_hi, proj["v"][:]).then_inc(v_hi_done, 1)

            def og_high(a):
                act.wait_ge(o_gated, K * (a + 1))
                nc.scalar.copy(og_hi, og).then_inc(og_hi_done, 1)

            def y_copy(a):
                for k in range(K):
                    act.wait_ge(wo_mm, K * a + k + 1)
                    if a:
                        act.wait_ge(ln_xc, NORM["o0"] + 1)
                    nc.scalar.copy(ysb[:, k, :], A[k][:]).then_inc(y_out, 1)

            norm(0)
            h_high(0)
            w_high(0)
            route(0)
            for s in range(STEPS):
                p, t = divmod(s, TILES)
                if s + 1 < STEPS:
                    w_high(s + 1)
                tile(s)
                tile_high(s)
                if s == 0:
                    route_out(0)
                if p == 0:
                    if t == AT_SPLIT:
                        act.wait_ge(aw_loaded, 16)
                        nc.scalar.copy(aw_hi[:], aw_raw).then_inc(aw_hi_done, 1)
                    if t == AT_LN_NEXT:
                        norm(NORM["f1"])
                        h_high(1)
                    if t == AT_ROUTE_NEXT:
                        route(1)
                        route_out(1)
                if p in (1, 2):
                    a = p - 1
                    if t == AT_ATT_LN:
                        norm(NORM[f"a{a}"])
                    if AT_PROJ <= t < AT_PROJ + len(MIX):
                        m = t - AT_PROJ
                        mix_high(a, m)
                        project_out(a, m)
                        if m == len(MIX) - 1:
                            v_high(a)
                    if t == AT_POST:
                        og_high(a)
                        y_copy(a)
                    if t == AT_OUT_LN:
                        norm(NORM[f"o{a}"])
                    if t == AT_FFN_LN:
                        norm(NORM[f"f{p + 1}"])
                        h_high(p + 1)
                    if t == AT_ROUTE:
                        route(p + 1)
                        route_out(p + 1)

        @block.vector
        def _(dve):
            steps = [0]

            def link(ins):
                steps[0] += 1
                ins.then_inc(route_step, 1)
                dve.wait_ge(route_step, steps[0])

            def norm(n, src, dst):
                dve.wait_ge(ln_mean, n + 1)
                if n:
                    dve.wait_ge(ln_sq, n)
                    dve.wait_ge(ln_h, n)
                nc.vector.tensor_tensor(xc[:], src, over_k(A[0][:]), ALU.subtract).then_inc(ln_xc, 1)
                dve.wait_ge(ln_sd, n + 1)
                nc.vector.reciprocal(rstd[:], sd[:]).then_inc(ln_rstd, 1)
                dve.wait_ge(ln_rstd, n + 1)
                dve.wait_ge(ln_xc, n + 1)
                dve.wait_ge(ln_sq, n + 1)
                nc.vector.tensor_tensor(dst, xc[:], over_k(rstd[:]), ALU.mult).then_inc(ln_h, 1)

            def ffn_norm(p):
                if p:
                    dve.wait_ge(logits_done, p)
                    dve.wait_ge(h_hi_done, p)
                    dve.wait_ge(h_lo_done, p)
                if p == 0:
                    dve.wait_ge(x_loaded[0], 16)
                elif p == 1:
                    dve.wait_ge(x_loaded[1], 16)
                else:
                    dve.wait_ge(att_added, K * (p - 1))
                norm(NORM[f"f{p}"], half_x(p % HALVES), hf[:])
                dve.wait_ge(h_hi_done, p + 1)
                if p >= 2:
                    dve.wait_ge(u_done, (p - 1) * TILES)
                nc.vector.tensor_tensor(h_lo[:, p % 2], hf[:], h_hi[:, p % 2].bitcast(F32),
                                        ALU.subtract).then_inc(h_lo_done, 1)

            def top(values, thr, k, resets, out, t1, t2, cnt):
                n = values.shape[2]
                wide = thr.unsqueeze(2).broadcast_to([P, TT, n])
                flat = "p t n -> p (t n)"
                link(nc.vector.tensor_tensor(out, values, wide, ALU.is_gt))
                link(nc.vector.tensor_tensor(t1, values, wide, ALU.is_equal))
                link(nc.vector.tensor_reduce(cnt, out, AX_X, ALU.add))
                link(nc.vector.tensor_scalar(cnt, cnt, -1.0, float(k), ALU.mult, ALU.add))
                link(nc.vector.tensor_tensor_scan(t2.rearrange(flat), resets, t1.rearrange(flat), 0.0,
                                                  ALU.mult, ALU.add))
                link(nc.vector.tensor_tensor(t2, t2, cnt.unsqueeze(2).broadcast_to([P, TT, n]), ALU.is_le))
                link(nc.vector.tensor_tensor(t1, t1, t2, ALU.mult))
                link(nc.vector.tensor_tensor(out, out, t1, ALU.add))

            def route(p):
                dve.wait_ge(tanh_done, p + 1)
                link(nc.vector.tensor_scalar(score[:], score[:], 0.5, 0.5, ALU.mult, ALU.add))
                link(nc.vector.tensor_tensor(choice[:], score[:], bias.unsqueeze(1).broadcast_to([P, TT, E]),
                                             ALU.add))
                by_two = choice[:].rearrange("p t (g a b) -> p (t g) a b", g=GROUPS, b=2)
                link(nc.vector.tensor_tensor(pair[:, 0], by_two[:, :, :, 0], by_two[:, :, :, 1], ALU.max))
                link(nc.vector.tensor_tensor(pair[:, 1], by_two[:, :, :, 0], by_two[:, :, :, 1], ALU.min))
                flat4 = [g4[:, i].rearrange("p t g -> p (t g)") for i in range(8)]
                link(nc.vector.tensor_tensor(flat4[0], pair[:, 0, :, 0], pair[:, 0, :, 1], ALU.max))
                link(nc.vector.tensor_tensor(flat4[1], pair[:, 0, :, 0], pair[:, 0, :, 1], ALU.min))
                link(nc.vector.tensor_tensor(flat4[2], pair[:, 1, :, 0], pair[:, 1, :, 1], ALU.max))
                link(nc.vector.tensor_tensor(flat4[1], flat4[1], flat4[2], ALU.max))
                link(nc.vector.tensor_tensor(flat4[3], flat4[0], flat4[1], ALU.add))
                gs = g4[:, 3]
                a, b, c, d = (gs[:, :, i] for i in range(GROUPS))
                hi1, lo1, hi2, lo2, thr, cnt = (g1[:, i] for i in range(6))
                link(nc.vector.tensor_tensor(hi1, a, b, ALU.max))
                link(nc.vector.tensor_tensor(lo1, a, b, ALU.min))
                link(nc.vector.tensor_tensor(hi2, c, d, ALU.max))
                link(nc.vector.tensor_tensor(lo2, c, d, ALU.min))
                link(nc.vector.tensor_tensor(lo1, lo1, lo2, ALU.max))
                link(nc.vector.tensor_tensor(hi1, hi1, hi2, ALU.min))
                link(nc.vector.tensor_tensor(thr, hi1, lo1, ALU.max))
                top(gs, thr, TOP_GROUPS, cst[:, C_RSTG:C_RSTG + TT * GROUPS], g4[:, 4], g4[:, 5], g4[:, 6], cnt)
                in_group = g4[:, 4].rearrange("p t g -> p (t g)").unsqueeze(2).broadcast_to(
                    [P, TT * GROUPS, E // GROUPS])
                link(nc.vector.tensor_tensor(rt[:, 0].rearrange("p t (g i) -> p (t g) i", g=GROUPS),
                                             choice[:].rearrange("p t (g i) -> p (t g) i", g=GROUPS),
                                             in_group, ALU.mult))
                for tt in range(TT):
                    ins = nc.vector.max(out=top8[:, tt, :], in_=rt[:, 0, tt, :])
                    link(ins)
                top(rt[:, 0], top8[:, :, TOP_K - 1], TOP_K, cst[:, C_RSTE:C_RSTE + TT * E],
                    rt[:, 1], rt[:, 2], rt[:, 3], cnt)
                link(nc.vector.tensor_tensor(rt[:, 4], rt[:, 1], score[:], ALU.mult))
                link(nc.vector.tensor_reduce(cnt, rt[:, 4], AX_X, ALU.add))
                link(nc.vector.tensor_scalar(cnt, cnt, 1e-20, None, ALU.add))
                link(nc.vector.reciprocal(g1[:, 6], cnt))
                link(nc.vector.tensor_tensor(rt[:, 3], rt[:, 4],
                                             g1[:, 6].unsqueeze(2).broadcast_to([P, TT, E]), ALU.mult))
                link(nc.vector.tensor_scalar(rt[:, 4], rt[:, 3], ROUTE_SCALE, None, ALU.mult))
                if p:
                    dve.wait_ge(comb_tr, p)
                link(nc.vector.tensor_copy(comb2[:, :, 0, :], rt[:, 4]))
                nc.vector.tensor_tensor(comb2[:, :, 1, :], rt[:, 4], comb2[:, :, 0, :].bitcast(F32),
                                        ALU.subtract).then_inc(comb_done, 1)

            def tile(s):
                dve.wait_ge(sil_done, s + 1)
                dve.wait_ge(u_done, s + 1)
                if s >= BR:
                    dve.wait_ge(in_lo_done, s - BR + 1)
                b = inter[:, s % BR, :]
                nc.vector.tensor_tensor(b, sil[:, s % BR, :], U[:], ALU.mult).then_inc(up_done, 1)
                if is_expert(s):
                    dve.wait_ge(up_done, s + 1)
                    dve.wait_ge(cb_done, experts_before(s) + 1)
                    nc.vector.tensor_tensor(b, b, CB[:], ALU.mult).then_inc(scaled_done, 1)

            def add_ffn(p):
                dve.wait_ge(down_done, (p + 1) * TILES)
                xh = half_x(p % HALVES)
                nc.vector.scalar_tensor_tensor(out=xh, in0=Y[:], scalar=0.5, in1=xh, op0=ALU.mult,
                                               op1=ALU.add).then_inc(ffn_added, 1)

            def shift(a):
                h4 = ha[:].rearrange("p k (b t) -> p (k b) t", t=SEQ)
                x4 = xx[:].rearrange("p k (b t) -> p (k b) t", t=SEQ)
                dve.wait_ge(ln_h, NORM[f"a{a}"] + 1)
                nc.vector.tensor_tensor(x4[:, :, 1:SEQ], h4[:, :, 0:SEQ - 1], h4[:, :, 1:SEQ],
                                        ALU.subtract).then_inc(xx_done, 1)
                nc.vector.tensor_tensor(x4[:, :, 0:1], h4[:, :, 1:2], h4[:, :, 0:1],
                                        ALU.subtract).then_inc(xx_done, 1)

            def mix(a, m):
                i = len(MIX) * a + m
                dve.wait_ge(xx_done, 2 * (a + 1))
                if i >= 2:
                    dve.wait_ge(xm_lo_done, i - 1)
                if m == 1 and a:
                    dve.wait_ge(og_hi_done, a)
                    dve.wait_ge(og_lo_done, a)
                for k in range(K):
                    nc.vector.scalar_tensor_tensor(
                        out=xm[:, m % 2, k, :], in0=xx[:, k, :], scalar=par(f"tm_{MIX[m]}", k),
                        in1=ha[:, k, :], op0=ALU.mult, op1=ALU.add).then_inc(xm_done, 1)
                dve.wait_ge(xm_hi_done, i + 1)
                dve.wait_ge(xm_done, 2 * (i + 1))
                nc.vector.tensor_tensor(xm_lo[:, m % 2], xm[:, m % 2], xm_hi[:, m % 2].bitcast(F32),
                                        ALU.subtract).then_inc(xm_lo_done, 1)

            def before_units(a):
                dve.wait_ge(proj_out, K * len(MIX) * (a + 1))
                nc.vector.tensor_scalar(proj["g"][:], proj["g"][:], 0.5, 0.5, ALU.mult,
                                        ALU.add).then_inc(gate_sig, 1)
                for k in range(K):
                    nc.vector.scalar_tensor_tensor(
                        out=xx[:, k, :], in0=proj["r"][:, k, :], scalar=par("time_first", k),
                        in1=proj["k"][:, k, :], op0=ALU.mult, op1=ALU.mult).then_inc(ruk_done, 1)
                dve.wait_ge(v_hi_done, a + 1)
                nc.vector.tensor_tensor(v_lo, proj["v"][:], v_hi.bitcast(F32), ALU.subtract).then_inc(v_lo_done, 1)
                dve.wait_ge(ruk_done, K * (a + 1))
                nc.vector.memset(proj["r"][:].rearrange("p k (b t) -> p (k b) t", t=SEQ)[:, :, 0:1],
                                 0.0).then_inc(r_masked, 1)
                for k in range(K):
                    dve.wait_ge(diag_mm, K * a + k + 1)
                    nc.vector.tensor_tensor(ha[:, k, :], A[k][:], proj["v"][:, k, :],
                                            ALU.mult).then_inc(diag_v, 1)

            def add_diag(a, k):
                i = K * a + k
                dve.wait_ge(red_done, UNITS * a + D * (k + 1))
                dve.wait_ge(diag_v, i + 1)
                nc.vector.tensor_tensor(ysb[:, k, :], O[:], ha[:, k, :], ALU.add).then_inc(o_added, 1)
                dve.wait_ge(o_added, i + 1)
                dve.wait_ge(gate_sig, a + 1)
                nc.vector.tensor_tensor(og[:, k, :], ysb[:, k, :], proj["g"][:, k, :],
                                        ALU.mult).then_inc(o_gated, 1)

            def unit(a, n):
                i = UNITS * a + n
                k, j = divmod(n, D)
                dve.wait_ge(vb_done, i + 1)
                if i >= 2:
                    dve.wait_ge(scan_done, i - 1)
                nc.vector.tensor_tensor(kv[:, i % 2, :], proj["k"][:, k, :], A[n % 2][:],
                                        ALU.mult).then_inc(kv_done, 1)
                dve.wait_ge(kv_done, i + 1)
                if i >= 2:
                    dve.wait_ge(rs_done, i - 1)
                nc.vector.tensor_tensor_scan(state[:, i % 2, 1:N + 1], decay_t[:, k, :], kv[:, i % 2, :],
                                             0.0, ALU.mult, ALU.add).then_inc(scan_done, 1)
                dve.wait_ge(scan_done, i + 1)
                dve.wait_ge(r_masked, a + 1)
                if i >= PR:
                    dve.wait_ge(red_done, i - PR + 1)
                nc.vector.tensor_tensor(rs[:, i % PR, :], proj["r"][:, k, :], state[:, i % 2, 0:N],
                                        ALU.mult).then_inc(rs_done, 1)

            def out_norm(a):
                dve.wait_ge(y_out, K * (a + 1))
                norm(NORM[f"o{a}"], ysb, xx[:])
                dve.wait_ge(ln_h, NORM[f"o{a}"] + 1)
                for k in range(K):
                    nc.vector.tensor_scalar(ha[:, k, :], xx[:, k, :], par("ln_w", k), par("ln_b", k),
                                            ALU.mult, ALU.add).then_inc(z_step, 1)
                dve.wait_ge(z_step, K * (a + 1))
                for k in range(K):
                    xk = x[:, k, a * N:(a + 1) * N]
                    nc.vector.tensor_tensor(xk, xk, ha[:, k, :], ALU.add).then_inc(att_added, 1)

            dve.wait_ge(c_loaded, 16)
            dve.wait_ge(decay_done, 1)
            dve.wait_ge(dt_set, 2)
            for k in range(K):
                nc.vector.tensor_scalar(decay_t[:, k, :], decay_t[:, k, :], decay[:, k:k + 1], None,
                                        ALU.mult).then_inc(dt_done, 1)
            ffn_norm(0)
            for s in range(STEPS):
                p, t = divmod(s, TILES)
                tile(s)
                if s == 0:
                    route(0)
                if t == 0 and p:
                    add_ffn(p - 1)
                if p == 0:
                    if t == AT_SPLIT:
                        dve.wait_ge(aw_hi_done, 1)
                        nc.vector.tensor_tensor(aw_lo[:], aw_raw, aw_hi[:].bitcast(F32),
                                                ALU.subtract).then_inc(aw_lo_done, 1)
                    if t == AT_LN_NEXT:
                        ffn_norm(1)
                    if t == AT_ROUTE_NEXT:
                        route(1)
                if p in (1, 2):
                    a = p - 1
                    if t == AT_ATT_LN:
                        dve.wait_ge(ffn_added, a + 1)
                        if a:
                            dve.wait_ge(z_step, K * a)
                        norm(NORM[f"a{a}"], half_x(a), ha[:])
                        if a:
                            dve.wait_ge(z_step, K * a)
                        shift(a)
                    if AT_PROJ <= t < AT_PROJ + len(MIX):
                        mix(a, t - AT_PROJ)
                    if t == AT_UNITS:
                        dve.wait_ge(dt_done, K)
                        dve.wait_ge(state0_set, 1)
                        before_units(a)
                    for n in units_of(p, t):
                        if n < UNITS:
                            unit(a, n)
                        if n == D + 1:
                            add_diag(a, 0)
                    if t == AT_POST:
                        add_diag(a, 1)
                        dve.wait_ge(og_hi_done, a + 1)
                        dve.wait_ge(o_gated, K * (a + 1))
                        nc.vector.tensor_tensor(og_lo, og, og_hi.bitcast(F32),
                                                ALU.subtract).then_inc(og_lo_done, 1)
                    if t == AT_OUT_LN:
                        out_norm(a)
                    if t == AT_FFN_LN:
                        ffn_norm(p + 1)
                    if t == AT_ROUTE:
                        route(p + 1)
            add_ffn(PASSES - 1)

        @block.tensor
        def _(pe):
            def three(out, w_h, w_l, m_h, m_l, first, last):
                nc.tensor.matmul(out, w_h, m_h, start=first, stop=False)
                nc.tensor.matmul(out, w_l, m_h, start=False, stop=False)
                return nc.tensor.matmul(out, w_h, m_l, start=False, stop=last)

            def norm(n, src):
                for k in range(K):
                    mm = nc.tensor.matmul(A[0][:], ones_c, src[:, k, :], start=(k == 0), stop=(k == K - 1))
                mm.then_inc(ln_mean, 1)
                pe.wait_ge(ln_sq, n + 1)
                for k in range(K):
                    mm = nc.tensor.matmul(A[1][:], ones_c, sq[:, k, :], start=(k == 0), stop=(k == K - 1))
                mm.then_inc(ln_var, 1)

            def logits(p):
                pe.wait_ge(ln_h, NORM[f"f{p}"] + 1)
                for tt in range(TT):
                    for k in range(K):
                        mm = nc.tensor.matmul(A[0][:, tt * E:(tt + 1) * E], hf[:, k, tt * P:(tt + 1) * P],
                                              gate_t[:, k, :], start=(k == 0), stop=(k == K - 1))
                mm.then_inc(logits_done, 1)

            def turn_comb(p):
                pe.wait_ge(ln_sd, NORM[f"f{p}"] + 1)
                pe.wait_ge(comb_done, p + 1)
                for tt in range(TT):
                    mm = nc.tensor.transpose(A[1][0:2 * E, tt * P:(tt + 1) * P],
                                             comb2[:, tt].rearrange("p h e -> p (h e)").bitcast(F32), ident)
                mm.then_inc(comb_tr, 1)

            def gate_up(s):
                p = s // TILES
                pe.wait_ge(w_lo_done, s + 1)
                if s % TILES == 0:
                    pe.wait_ge(h_hi_done, p + 1)
                    pe.wait_ge(h_lo_done, p + 1)
                for gu, (bank, done, free) in enumerate(((G, g_done, sil_done), (U, u_done, up_done))):
                    if s:
                        pe.wait_ge(free, s)
                    for k in range(K):
                        at = (gu * K + k) * P
                        mm = three(bank[:], w_hi[:, s % WR, at:at + P], w_lo[:, s % WR, at:at + P],
                                   h_hi[:, p % 2, k, :], h_lo[:, p % 2, k, :], k == 0, k == K - 1)
                    mm.then_inc(done, 1)

            def spread_comb(s):
                p, t = divmod(s, TILES)
                if t < SHARED_TILES:
                    return
                if t == SHARED_TILES:
                    pe.wait_ge(comb_t_done, p + 1)
                if experts_before(s):
                    pe.wait_ge(scaled_done, experts_before(s))
                nc.tensor.matmul(CB[:], sel_e[:, t - SHARED_TILES, :], comb_t[:, p % 2, :], start=True,
                                 stop=True).then_inc(cb_done, 1)

            def down(s):
                p, t = divmod(s, TILES)
                pe.wait_ge(in_hi_done, s + 1)
                pe.wait_ge(in_lo_done, s + 1)
                if t == 0 and p:
                    pe.wait_ge(ffn_added, p)
                for c in range(K):
                    at = 2 * K * P + c * P
                    mm = three(Y[:, c, :], w_hi[:, s % WR, at:at + P], w_lo[:, s % WR, at:at + P],
                               in_hi[:, s % BR, :], in_lo[:, s % BR, :], t == 0, t == TILES - 1)
                mm.then_inc(down_done, 1)

            def project(a, m):
                i = len(MIX) * a + m
                pe.wait_ge(xm_hi_done, i + 1)
                pe.wait_ge(xm_lo_done, i + 1)
                for c in range(K):
                    if m:
                        pe.wait_ge(proj_out, K * (i - 1) + c + 1)
                    for k in range(K):
                        cols = slice(c * P, (c + 1) * P)
                        mm = three(A[c][:], aw_hi[:, m, k, cols], aw_lo[:, m, k, cols],
                                   xm_hi[:, m % 2, k, :], xm_lo[:, m % 2, k, :], k == 0, k == K - 1)
                    mm.then_inc(proj_mm, 1)

            def diag(a):
                pe.wait_ge(ruk_done, K * (a + 1))
                for k in range(K):
                    pe.wait_ge(proj_out, K * len(MIX) * (a + 1))
                    nc.tensor.matmul(A[k][:], head_ones, xx[:, k, :], start=True, stop=True).then_inc(diag_mm, 1)

            def spread_v(a, n):
                i = UNITS * a + n
                k, j = divmod(n, D)
                if n < 2:
                    pe.wait_ge(diag_v, K * (a + 1))
                else:
                    pe.wait_ge(kv_done, i - 1)
                nc.tensor.matmul(A[n % 2][:], sel_j[:, j, :], v_hi[:, k, :], start=True, stop=False)
                nc.tensor.matmul(A[n % 2][:], sel_j[:, j, :], v_lo[:, k, :], start=False,
                                 stop=True).then_inc(vb_done, 1)

            def reduce(a, n):
                i = UNITS * a + n
                k, j = divmod(n, D)
                pe.wait_ge(rs_done, i + 1)
                if j == 0 and K * a + k:
                    pe.wait_ge(o_added, K * a + k)
                nc.tensor.matmul(O[:], red_j(j), rs[:, i % PR, :], start=(j == 0),
                                 stop=(j == D - 1)).then_inc(red_done, 1)

            def out_project(a):
                pe.wait_ge(og_hi_done, a + 1)
                pe.wait_ge(og_lo_done, a + 1)
                pe.wait_ge(kv_done, UNITS * (a + 1))
                for c in range(K):
                    for k in range(K):
                        cols = slice(c * P, (c + 1) * P)
                        mm = three(A[c][:], aw_hi[:, 4, k, cols], aw_lo[:, 4, k, cols],
                                   og_hi[:, k, :], og_lo[:, k, :], k == 0, k == K - 1)
                    mm.then_inc(wo_mm, 1)

            pe.wait_ge(c_loaded, 16)
            pe.wait_ge(x_loaded[0], 16)
            norm(0, half_x(0))
            logits(0)
            pe.wait_ge(sel_loaded, 32)
            for s in range(STEPS + 1):
                p, t = divmod(s, TILES)
                if s < STEPS:
                    gate_up(s)
                    if s == 1:
                        turn_comb(0)
                    spread_comb(s)
                if s:
                    down(s - 1)
                if s == STEPS:
                    break
                if p == 0:
                    if t == AT_LN_NEXT:
                        pe.wait_ge(x_loaded[1], 16)
                        pe.wait_ge(tanh_done, 1)
                        pe.wait_ge(comb_t_done, 1)
                        norm(NORM["f1"], half_x(1))
                    if t == AT_ROUTE_NEXT:
                        logits(1)
                        turn_comb(1)
                if p in (1, 2):
                    a = p - 1
                    if t == AT_ATT_LN:
                        pe.wait_ge(ffn_added, a + 1)
                        pe.wait_ge(tanh_done, p + a)
                        pe.wait_ge(comb_t_done, p + a)
                        norm(NORM[f"a{a}"], half_x(a))
                    if AT_PROJ <= t < AT_PROJ + len(MIX):
                        if t == AT_PROJ:
                            pe.wait_ge(ln_sd, NORM[f"a{a}"] + 1)
                            pe.wait_ge(aw_lo_done, 1)
                        project(a, t - AT_PROJ)
                    if t == AT_UNITS:
                        diag(a)
                        pe.wait_ge(v_hi_done, a + 1)
                        pe.wait_ge(v_lo_done, a + 1)
                    for n in units_of(p, t):
                        if n < UNITS:
                            spread_v(a, n)
                        if n >= 2:
                            reduce(a, n - 2)
                    if t == AT_POST:
                        out_project(a)
                    if t == AT_OUT_LN:
                        pe.wait_ge(y_out, K * (a + 1))
                        norm(NORM[f"o{a}"], ysb)
                    if t == AT_FFN_LN:
                        pe.wait_ge(ln_sd, NORM[f"o{a}"] + 1)
                        pe.wait_ge(att_added, K * (a + 1))
                        norm(NORM[f"f{p + 1}"], half_x((p + 1) % HALVES))
                    if t == AT_ROUTE:
                        logits(p + 1)
                        turn_comb(p + 1)


def constants():
    c = np.zeros((P, C_END), np.float32)
    c[:, C_ONES:C_ONES + P] = 1.0 / C
    head = np.arange(P) // D
    c[:, C_HEAD:C_HEAD + P] = head[:, None] == head[None, :]
    c[:, C_IDENT:C_IDENT + P] = np.eye(P)
    sel = np.zeros((P, D, P), np.float32)
    for j in range(D):
        sel[:, j, :] = (head[:, None] == head[None, :]) & (np.arange(P) % D == j)[:, None]
        c[:, C_RED + j * P:C_RED + (j + 1) * P] = sel[:, j, :].T
    c[:, C_RSTE:C_RSTE + TT * E] = np.arange(TT * E) % E != 0
    c[:, C_RSTG:C_RSTG + TT * GROUPS] = np.arange(TT * GROUPS) % GROUPS != 0
    unit_expert = np.arange(E * I) // I
    exp = (np.arange(2 * E) % E)[:, None] == unit_expert[None, :]
    return c, sel, exp.astype(np.float32).reshape(2 * E, EXPERT_TILES, P)


def kernel(**inputs):
    import concourse.bacc as bacc
    from concourse.bass_utils import run_bass_kernel_spmd

    a = {n.removeprefix("L0_"): np.asarray(v) for n, v in inputs.items()}

    x = np.ascontiguousarray(a["attn_x"].reshape(TOKENS, K, P).transpose(2, 1, 0))

    pad = np.zeros((SHARED_TILES * P - I * N_SHARED, C), np.float32)

    def rows(shared, routed):
        return np.concatenate([shared, pad, routed.reshape(E * I, C)])

    gate = rows(a["ffn_shared_gate_w"], a["ffn_gate_proj"]).reshape(TILES, P, K, P).transpose(0, 3, 2, 1)
    up = rows(a["ffn_shared_up_w"], a["ffn_up_proj"]).reshape(TILES, P, K, P).transpose(0, 3, 2, 1)
    down = rows(a["ffn_shared_down_w"].T, a["ffn_down_proj"].transpose(0, 2, 1)).reshape(TILES, P, C)
    w = np.concatenate([gate.reshape(TILES, P, K * P), up.reshape(TILES, P, K * P), down], axis=2)

    aw = np.stack([a[f"attn_W{m}"].T.reshape(K, P, C).transpose(1, 0, 2) for m in (*MIX, "o")], axis=1)

    c, sel, exp = constants()
    c[:, C_GATE:C_GATE + K * E] = a["ffn_gate_weight"].T.reshape(K, P, E).transpose(1, 0, 2).reshape(P, K * E)
    c[:, C_BIAS:C_BIAS + E] = a["ffn_e_score_correction_bias"]
    for n, name in enumerate(PARAMS):
        c[:, C_PAR + K * n:C_PAR + K * (n + 1)] = a[f"attn_{name}"].reshape(K, P).T

    nc = bacc.Bacc("TRN2", target_bir_lowering=False, num_devices=1)
    arrays, args = {}, []
    for name, v in (("x", x), ("w", w), ("aw", aw), ("consts", c), ("sel", sel), ("exp", exp)):
        v = np.ascontiguousarray(v)
        arrays[f"in_{name}_dram"] = v
        args.append(nc.dram_tensor(f"in_{name}_dram", v.shape, mybir.dt.from_np(v.dtype), kind="ExternalInput").ap())
    args.append(nc.dram_tensor("out_0_dram", (P, K, TOKENS), F32, kind="ExternalOutput").ap())
    macaron(nc, *args)
    r = run_bass_kernel_spmd(nc, [arrays], core_ids=[0])
    out = r.results[0]["out_0_dram"]
    return np.ascontiguousarray(out.transpose(2, 1, 0)).reshape(BATCH, SEQ, C)
```

```python
from contextlib import ExitStack

import concourse.bass as bass
import numpy as np
from concourse import mybir

F32 = mybir.dt.float32
F32R = mybir.dt.float32r
ALU = mybir.AluOpType
ACT = mybir.ActivationFunctionType
AX_X = mybir.AxisListType.X

P = 128
BATCH, SEQ, C = 4, 256, 256
TOKENS = BATCH * SEQ
HALVES = 2
N = TOKENS // HALVES
HB = BATCH // HALVES
K = C // P
HEADS, D = 16, 16
E, I, GROUPS, TOP_GROUPS, TOP_K, N_SHARED = 16, 176, 4, 2, 6, 2
ROUTE_SCALE = 2.5
EPS = 1e-5
SHARED_TILES = -(-I * N_SHARED // P)
EXPERT_TILES = E * I // P
TILES = SHARED_TILES + EXPERT_TILES
PASSES = 2 * HALVES
STEPS = PASSES * TILES
WCOLS = 2 * K * P + C
TT = N // P
UNITS = K * D

RAW, WR, BR, PR, VR, SR = 3, 3, 2, 3, 4, 3

C_ONES, C_HEAD, C_IDENT, C_GATE = 0, P, 2 * P, 3 * P
C_BIAS = C_GATE + K * E
C_RSTE = C_BIAS + E
C_RSTG = C_RSTE + TT * E
C_PAR = C_RSTG + TT * GROUPS
PARAMS = ("time_decay", "time_first", "tm_v", "tm_k", "tm_r", "tm_g", "ln_w", "ln_b")
C_END = C_PAR + K * len(PARAMS)
MIX = ("v", "k", "r", "g")

AT_SPLIT, AT_NORM_B = 5, 8
AT_NORM_A, AT_MIX, AT_PREP, AT_UNITS = 1, 3, 6, 7
SLOTS_PER_STEP, SCAN_LAG, READ_LAG, SUM_LAG = 3, 1, 2, 4
SLOTS = UNITS + SUM_LAG
V_AHEAD = 4
AT_OUT = AT_UNITS + -(-SLOTS // SLOTS_PER_STEP)
AT_NORM_O, AT_NORM_F = AT_OUT + 1, AT_OUT + 3
assert AT_NORM_F + 2 < TILES


def route_part(s, part):
    for p, first in ((1, AT_NORM_B + 2), (2, TILES + AT_NORM_F + 2), (3, 2 * TILES + AT_NORM_F + 2)):
        if s == first + part:
            return p
    if s == part:
        return 0
    return None


NORM = {"f0": 0, "f1": 1, "a0": 2, "o0": 3, "f2": 4, "a1": 5, "o1": 6, "f3": 7}


def macaron(nc, x_d, w_d, aw_d, c_d, sel_d, exp_d, out_d):
    ctx = ExitStack()
    with ctx:
        def sb(name, shape, dt=F32):
            return ctx.enter_context(nc.sbuf_tensor(name, shape, dt))

        def pb(name, shape):
            return ctx.enter_context(nc.psum_tensor(name, shape, F32))

        def sem(name):
            return ctx.enter_context(nc.semaphore(name))

        cst = sb("cst", [P, C_END])
        sum_j = sb("sum_j", [P, D, P])
        sel_e = sb("sel_e", [2 * E, EXPERT_TILES, P], F32R)
        ones_c = cst[:, C_ONES:C_ONES + P]
        head_ones = cst[:, C_HEAD:C_HEAD + P]
        ident = cst[:, C_IDENT:C_IDENT + P]
        gate_t = cst[:, C_GATE:C_GATE + K * E].rearrange("p (k e) -> p k e", k=K)
        bias = cst[:, C_BIAS:C_BIAS + E]

        def par(name, k):
            at = C_PAR + K * PARAMS.index(name) + k
            return cst[:, at:at + 1]

        eps = sb("eps", [P, 1])
        lam = sb("lam", [P, K])
        decay = sb("decay", [P, K])
        decay_t = sb("decay_t", [P, K, N])
        early = sb("early", [P, (2 + PR) * N])
        assert (2 + PR) * N == 5 * K * C
        aw_raw = early[:].rearrange("p (m k c) -> p m k c", m=5, k=K)
        aw_hi = sb("aw_hi", [P, 5, K, C], F32R)
        aw_lo = sb("aw_lo", [P, 5, K, C], F32R)
        x = sb("x", [P, K, TOKENS])
        w_raw = sb("w_raw", [P, RAW, WCOLS])
        w_hi = sb("w_hi", [P, WR, WCOLS], F32R)
        w_lo = sb("w_lo", [P, WR, WCOLS], F32R)
        hf = sb("hf", [P, K, N])
        h_hi = sb("h_hi", [P, 2, K, N], F32R)
        h_lo = sb("h_lo", [P, 2, K, N], F32R)
        sil = sb("sil", [P, BR, N])
        inter = sb("inter", [P, BR, N])
        in_hi = sb("in_hi", [P, BR, N], F32R)
        in_lo = sb("in_lo", [P, BR, N], F32R)
        xc = sb("xc", [P, K, N])
        sq = sb("sq", [P, K, N])
        var_t = sb("var_t", [P, N // 32, 32])
        sd = sb("sd", [P, N // 32])
        rsd = sb("rsd", [P, N // 32])
        rstd = sb("rstd", [P, N])
        score = sb("score", [P, TT, E])
        choice = sb("choice", [P, TT, E])
        pair = sb("pair", [P, 2, TT * GROUPS, 2])
        g4 = sb("g4", [P, 8, TT, GROUPS])
        g1 = sb("g1", [P, 8, TT])
        rt = sb("rt", [P, 5, TT, E])
        top8 = sb("top8", [P, TT, 8])
        comb2 = sb("comb2", [P, TT, 2, E], F32R)
        comb_t = sb("comb_t", [2 * E, 2, N], F32R)
        ha = sb("ha", [P, K, N])
        xx = sb("xx", [P, K, N])
        xm = sb("xm", [P, 2, K, N])
        xm_hi = sb("xm_hi", [P, 2, K, N], F32R)
        xm_lo = sb("xm_lo", [P, 2, K, N], F32R)
        proj = {m: sb(f"{m}_t", [P, K, N]) for m in MIX}
        vb = sb("vb", [P, VR, N])
        kv = early[:, 0:2 * N].rearrange("p (r t) -> p r t", r=2)
        state = sb("state", [P, SR, N + 1])
        rs = early[:, 2 * N:].rearrange("p (r t) -> p r t", r=PR)
        og, og_hi, og_lo = xm[:, 1], xm_hi[:, 1], xm_lo[:, 1]
        ysb = xm[:, 0]

        Y = pb("Y", [P, K, N])
        G = pb("G", [P, N])
        U = pb("U", [P, N])
        CB = pb("CB", [P, N])
        O = pb("O", [P, N])
        A = [pb("A0", [P, N]), pb("A1", [P, N])]

        c_loaded, aw_loaded, sel_loaded = sem("c_loaded"), sem("aw_loaded"), sem("sel_loaded")
        sum_loaded = sem("sum_loaded")
        x_loaded = [sem(f"x_loaded{half}") for half in range(HALVES)]
        w_loaded = [sem(f"w_loaded{i}") for i in range(RAW)]
        eps_set, lam_done, decay_done, dt_set, dt_done = (
            sem("eps_set"), sem("lam_done"), sem("decay_done"), sem("dt_set"), sem("dt_done"))
        state0_set = sem("state0_set")
        aw_hi_done, aw_lo_done = sem("aw_hi_done"), sem("aw_lo_done")
        ln_mean, ln_xc, ln_sq, ln_var, ln_turned, ln_sd, ln_rsd, ln_rstd, ln_h = (
            sem(n) for n in ("ln_mean", "ln_xc", "ln_sq", "ln_var", "ln_turned", "ln_sd", "ln_rsd",
                             "ln_rstd", "ln_h"))
        h_hi_done, h_lo_done = sem("h_hi_done"), sem("h_lo_done")
        w_hi_done, w_lo_done = sem("w_hi_done"), sem("w_lo_done")
        g_done, u_done, cb_done, down_done = sem("g_done"), sem("u_done"), sem("cb_done"), sem("down_done")
        sil_done, up_done, scaled_done = sem("sil_done"), sem("up_done"), sem("scaled_done")
        in_hi_done, in_lo_done, ffn_added = sem("in_hi_done"), sem("in_lo_done"), sem("ffn_added")
        logits_done, tanh_done, route_step, comb_done, comb_tr, comb_t_done = (
            sem(n) for n in ("logits_done", "tanh_done", "route_step", "comb_done", "comb_tr", "comb_t_done"))
        xx_done, xm_done, xm_hi_done, xm_lo_done, proj_mm, proj_out = (
            sem(n) for n in ("xx_done", "xm_done", "xm_hi_done", "xm_lo_done", "proj_mm", "proj_out"))
        gate_sig, ruk_done, r_masked, diag_mm, diag_v = (
            sem(n) for n in ("gate_sig", "ruk_done", "r_masked", "diag_mm", "diag_v"))
        vb_loaded = [sem(f"vb_loaded{i}") for i in range(VR)]
        kv_done, scan_done, rs_dve, rs_pool, red_done, o_added, o_gated = (
            sem(n) for n in ("kv_done", "scan_done", "rs_dve", "rs_pool", "red_done", "o_added", "o_gated"))
        og_hi_done, og_lo_done, wo_mm, y_out, z_step, att_added = (
            sem(n) for n in ("og_hi_done", "og_lo_done", "wo_mm", "y_out", "z_step", "att_added"))
        out_stored = sem("out_stored")

        block = ctx.enter_context(nc.Block())

        def half_x(half):
            return x[:, :, half * N:(half + 1) * N]

        def over_k(ap):
            return ap.unsqueeze(1).broadcast_to([P, K, N])

        def experts_before(s):
            return s // TILES * EXPERT_TILES + max(0, s % TILES - SHARED_TILES)

        def is_expert(s):
            return s % TILES >= SHARED_TILES

        def slots_of(p, t):
            if p not in (1, 2) or not AT_UNITS <= t < AT_OUT:
                return ()
            first = (t - AT_UNITS) * SLOTS_PER_STEP
            return tuple(n for n in range(first, first + SLOTS_PER_STEP) if n < SLOTS)

        def on_pool(i):
            return i % 3 != 0

        def wait_rs(eng, i):
            on_dve = i // 3 + 1
            if on_pool(i):
                eng.wait_ge(rs_pool, i + 1 - on_dve)
            else:
                eng.wait_ge(rs_dve, on_dve)

        def read_state(eng, i, k, done):
            eng.wait_ge(scan_done, i + 1)
            if i >= PR:
                eng.wait_ge(red_done, i - PR + 1)
            eng.tensor_tensor(rs[:, i % PR, :], proj["r"][:, k, :], state[:, i % SR, 0:N],
                              ALU.mult).then_inc(done, 1)

        @block.sync
        def _(sp):
            sp.dma_start(half_x(0), x_d[:, :, 0:N]).then_inc(x_loaded[0], 16)

            def load_vb(a, n):
                i = UNITS * a + n
                if n >= UNITS:
                    return
                k, j = divmod(n, D)
                if i >= VR:
                    sp.wait_ge(kv_done, i - VR + 1)
                rows = proj["v"][j::D, k, :]
                sp.dma_start(vb[:, i % VR, :], rows.unsqueeze(1).broadcast_to([P // D, D, N])).then_inc(
                    vb_loaded[i % VR], 16)

            for s in range(STEPS + V_AHEAD):
                vp, vt = divmod(s - V_AHEAD, TILES)
                if vp in (1, 2) and vt == AT_PREP:
                    sp.wait_ge(proj_out, K * (len(MIX) * (vp - 1) + 1))
                    for n in range(VR - 1):
                        load_vb(vp - 1, n)
                for n in slots_of(vp, vt):
                    load_vb(vp - 1, n + VR - 1)
                if s >= STEPS:
                    continue
                if s >= RAW:
                    sp.wait_ge(w_lo_done, s - RAW + 1)
                sp.dma_start(w_raw[:, s % RAW, :], w_d[s % TILES]).then_inc(w_loaded[s % RAW], 16)
                if s == 1:
                    sp.dma_start(half_x(1), x_d[:, :, N:TOKENS]).then_inc(x_loaded[1], 16)
                if s == 2:
                    sp.dma_start(aw_raw, aw_d).then_inc(aw_loaded, 16)
                if s == 3:
                    sp.dma_start(sum_j[:], sel_d).then_inc(sum_loaded, 16)
            for half in range(HALVES):
                sp.wait_ge(ffn_added, HALVES + half + 1)
                sp.dma_start(out_d[:, :, half * N:(half + 1) * N], half_x(half)).then_inc(out_stored, 16)
            sp.wait_ge(out_stored, 16 * HALVES)

        @block.gpsimd
        def _(pool):
            pool.dma_start(sel_e[:], exp_d).then_inc(sel_loaded, 16)
            nc.gpsimd.memset(eps[:], EPS).then_inc(eps_set, 1)
            nc.gpsimd.memset(state[:, :, 0:1], 0.0).then_inc(state0_set, 1)
            nc.gpsimd.memset(decay_t[:], 1.0).then_inc(dt_set, 1)
            pool.wait_ge(dt_set, 1)
            starts = decay_t[:].rearrange("p k (b t) -> p (k b) t", t=SEQ)[:, :, 0:1]
            nc.gpsimd.memset(starts, 0.0).then_inc(dt_set, 1)

            def split_w(s):
                pool.wait_ge(w_loaded[s % RAW], 16 * (s // RAW + 1))
                pool.wait_ge(w_hi_done, s + 1)
                if s >= WR:
                    pool.wait_ge(down_done, s - WR + 1)
                nc.gpsimd.tensor_tensor(w_lo[:, s % WR, :], w_raw[:, s % RAW, :],
                                        w_hi[:, s % WR, :].bitcast(F32), ALU.subtract).then_inc(w_lo_done, 1)

            def mix_low(a, m):
                i = len(MIX) * a + m
                pool.wait_ge(xm_done, 2 * (i + 1))
                pool.wait_ge(xm_hi_done, i + 1)
                if i >= 2:
                    pool.wait_ge(proj_mm, K * (i - 1))
                if m < 2 and a:
                    pool.wait_ge(wo_mm, K * a)
                nc.gpsimd.tensor_tensor(xm_lo[:, m % 2], xm[:, m % 2], xm_hi[:, m % 2].bitcast(F32),
                                        ALU.subtract).then_inc(xm_lo_done, 1)

            def slot(a, n):
                n -= READ_LAG
                i = UNITS * a + n
                if 0 <= n < UNITS and on_pool(i):
                    pool.wait_ge(r_masked, a + 1)
                    read_state(pool, i, n // D, rs_pool)

            def og_low(a):
                pool.wait_ge(og_hi_done, a + 1)
                nc.gpsimd.tensor_tensor(og_lo, og, og_hi.bitcast(F32), ALU.subtract).then_inc(og_lo_done, 1)

            split_w(0)
            split_w(1)
            for s in range(STEPS):
                p, t = divmod(s, TILES)
                a, slots = p - 1, slots_of(p, t)
                for n in slots[:2]:
                    slot(a, n)
                pool.wait_ge(in_hi_done, s + 1)
                if s >= BR:
                    pool.wait_ge(down_done, s - BR + 1)
                nc.gpsimd.tensor_tensor(in_lo[:, s % BR, :], inter[:, s % BR, :],
                                        in_hi[:, s % BR, :].bitcast(F32), ALU.subtract).then_inc(in_lo_done, 1)
                for n in slots[2:]:
                    slot(a, n)
                if s + 2 < STEPS:
                    split_w(s + 2)
                if p in (1, 2):
                    if AT_MIX <= t < AT_MIX + 2:
                        for m in (2 * (t - AT_MIX), 2 * (t - AT_MIX) + 1):
                            mix_low(a, m)
                    if t == AT_OUT - 1:
                        og_low(a)

        @block.scalar
        def _(act):
            act.dma_start(cst[:], c_d).then_inc(c_loaded, 16)
            act.wait_ge(c_loaded, 16)
            td = cst[:, C_PAR:C_PAR + K]
            nc.scalar.activation(lam[:], td, ACT.Exp).then_inc(lam_done, 1)
            act.wait_ge(lam_done, 1)
            nc.scalar.activation(decay[:], lam[:], ACT.Exp, scale=-1.0).then_inc(decay_done, 1)
            act.wait_ge(eps_set, 1)

            def norm_squares(n):
                act.wait_ge(ln_xc, n + 1)
                if n:
                    act.wait_ge(ln_var, n)
                nc.scalar.activation(sq[:], xc[:], ACT.Square).then_inc(ln_sq, 1)

            def norm_root(n):
                act.wait_ge(ln_turned, n + 1)
                if n:
                    act.wait_ge(ln_rsd, n)
                nc.scalar.activation(sd[:], var_t[:, :, 0], ACT.Sqrt, bias=eps[:, 0:1]).then_inc(ln_sd, 1)

            def h_high(p):
                act.wait_ge(ln_h, NORM[f"f{p}"] + 1)
                if p >= 2:
                    act.wait_ge(u_done, (p - 1) * TILES)
                nc.scalar.copy(h_hi[:, p % 2], hf[:]).then_inc(h_hi_done, 1)

            def route(p):
                act.wait_ge(logits_done, p + 1)
                if p:
                    act.wait_ge(comb_done, p)
                nc.scalar.activation(score[:], A[0][:, 0:TT * E].rearrange("p (t e) -> p t e", t=TT),
                                     ACT.Tanh, scale=0.5).then_inc(tanh_done, 1)

            def route_out(p):
                act.wait_ge(comb_tr, p + 1)
                if p >= 2:
                    act.wait_ge(cb_done, (p - 1) * EXPERT_TILES)
                nc.scalar.copy(comb_t[:, p % 2], A[1][0:2 * E, :]).then_inc(comb_t_done, 1)

            def w_high(s):
                act.wait_ge(w_loaded[s % RAW], 16 * (s // RAW + 1))
                if s >= WR:
                    act.wait_ge(down_done, s - WR + 1)
                nc.scalar.copy(w_hi[:, s % WR, :], w_raw[:, s % RAW, :]).then_inc(w_hi_done, 1)

            def tile(s):
                act.wait_ge(g_done, s + 1)
                if s >= BR:
                    act.wait_ge(up_done, s - BR + 1)
                nc.scalar.activation(sil[:, s % BR, :], G[:], ACT.Silu).then_inc(sil_done, 1)

            def tile_high(s):
                if is_expert(s):
                    act.wait_ge(scaled_done, experts_before(s) + 1)
                else:
                    act.wait_ge(up_done, s + 1)
                if s >= BR:
                    act.wait_ge(down_done, s - BR + 1)
                nc.scalar.copy(in_hi[:, s % BR, :], inter[:, s % BR, :]).then_inc(in_hi_done, 1)

            def mix_high(a, m):
                i = len(MIX) * a + m
                act.wait_ge(xm_done, 2 * (i + 1))
                if i >= 2:
                    act.wait_ge(proj_mm, K * (i - 1))
                if m < 2 and a:
                    act.wait_ge(wo_mm, K * a)
                nc.scalar.copy(xm_hi[:, m % 2], xm[:, m % 2]).then_inc(xm_hi_done, 1)

            def project_out(a, m):
                for k in range(K):
                    i = K * (len(MIX) * a + m) + k
                    act.wait_ge(proj_mm, i + 1)
                    if a:
                        act.wait_ge(o_gated, K)
                    func = ACT.Tanh if MIX[m] == "g" else ACT.Copy
                    nc.scalar.activation(proj[MIX[m]][:, k, :], A[k][:], func,
                                         scale=0.5 if MIX[m] == "g" else 1.0).then_inc(proj_out, 1)

            def og_high(a):
                act.wait_ge(o_gated, K * (a + 1))
                nc.scalar.copy(og_hi, og).then_inc(og_hi_done, 1)

            def y_copy(a):
                for k in range(K):
                    act.wait_ge(wo_mm, K * a + k + 1)
                    if a:
                        act.wait_ge(ln_xc, NORM["o0"] + 1)
                    nc.scalar.copy(ysb[:, k, :], A[k][:]).then_inc(y_out, 1)

            norm_squares(0)
            norm_root(0)
            h_high(0)
            w_high(0)
            w_high(1)
            route(0)
            for s in range(STEPS):
                p, t = divmod(s, TILES)
                a, slots = p - 1, slots_of(p, t)
                tile(s)
                if (q := route_part(s, 3)) is not None:
                    route_out(q)
                tile_high(s)
                if s + 2 < STEPS:
                    w_high(s + 2)
                if p == 0:
                    if t == AT_SPLIT:
                        act.wait_ge(aw_loaded, 16)
                        nc.scalar.copy(aw_hi[:], aw_raw).then_inc(aw_hi_done, 1)
                    if t == AT_NORM_B:
                        norm_squares(NORM["f1"])
                    if t == AT_NORM_B + 1:
                        norm_root(NORM["f1"])
                        h_high(1)
                if p in (1, 2):
                    if t == AT_NORM_A:
                        norm_squares(NORM[f"a{a}"])
                    if t == AT_NORM_A + 1:
                        norm_root(NORM[f"a{a}"])
                    if AT_MIX <= t <= AT_MIX + 2:
                        for m in (2 * (t - AT_MIX), 2 * (t - AT_MIX) + 1):
                            if t > AT_MIX:
                                project_out(a, m - 2)
                            if t < AT_MIX + 2:
                                mix_high(a, m)
                    if t == AT_OUT - 1:
                        og_high(a)
                    if t == AT_OUT:
                        y_copy(a)
                    if t == AT_NORM_O:
                        norm_squares(NORM[f"o{a}"])
                    if t == AT_NORM_O + 1:
                        norm_root(NORM[f"o{a}"])
                    if t == AT_NORM_F:
                        norm_squares(NORM[f"f{p + 1}"])
                    if t == AT_NORM_F + 1:
                        norm_root(NORM[f"f{p + 1}"])
                        h_high(p + 1)
                if s and (q := route_part(s, 0)) is not None:
                    route(q)

        @block.vector
        def _(dve):
            steps = [0]

            def link(ins):
                steps[0] += 1
                ins.then_inc(route_step, 1)
                dve.wait_ge(route_step, steps[0])

            def norm_center(n, src):
                dve.wait_ge(ln_mean, n + 1)
                if n:
                    dve.wait_ge(ln_sq, n)
                    dve.wait_ge(ln_h, n)
                nc.vector.tensor_tensor(xc[:], src, over_k(A[0][:]), ALU.subtract).then_inc(ln_xc, 1)

            def norm_scale(n, dst):
                dve.wait_ge(ln_var, n + 1)
                if n:
                    dve.wait_ge(ln_sd, n)
                nc.vector.transpose(var_t[:].rearrange("p a b -> p (a b)"), A[1][:]).then_inc(ln_turned, 1)
                dve.wait_ge(ln_sd, n + 1)
                if n:
                    dve.wait_ge(ln_rstd, n)
                nc.vector.reciprocal(rsd[:], sd[:]).then_inc(ln_rsd, 1)
                dve.wait_ge(ln_rsd, n + 1)
                if n:
                    dve.wait_ge(ln_h, n)
                nc.vector.transpose(rstd[:].rearrange("p (a b) -> p a b", b=32),
                                    rsd[:].unsqueeze(2).broadcast_to([P, N // 32, 32])).then_inc(ln_rstd, 1)
                dve.wait_ge(ln_rstd, n + 1)
                dve.wait_ge(ln_xc, n + 1)
                nc.vector.tensor_tensor(dst, xc[:], over_k(rstd[:]), ALU.mult).then_inc(ln_h, 1)

            def ffn_center(p):
                if p < 2:
                    dve.wait_ge(x_loaded[p], 16)
                else:
                    dve.wait_ge(att_added, K * (p - 1))
                norm_center(NORM[f"f{p}"], half_x(p % HALVES))

            def ffn_scale(p):
                if p:
                    dve.wait_ge(logits_done, p)
                    dve.wait_ge(h_hi_done, p)
                    dve.wait_ge(h_lo_done, p)
                norm_scale(NORM[f"f{p}"], hf[:])
                dve.wait_ge(h_hi_done, p + 1)
                if p >= 2:
                    dve.wait_ge(u_done, (p - 1) * TILES)
                nc.vector.tensor_tensor(h_lo[:, p % 2], hf[:], h_hi[:, p % 2].bitcast(F32),
                                        ALU.subtract).then_inc(h_lo_done, 1)

            def top(values, thr, k, resets, out, t1, t2, cnt):
                n = values.shape[2]
                wide = thr.unsqueeze(2).broadcast_to([P, TT, n])
                flat = "p t n -> p (t n)"
                link(nc.vector.tensor_tensor(out, values, wide, ALU.is_gt))
                link(nc.vector.tensor_tensor(t1, values, wide, ALU.is_equal))
                link(nc.vector.tensor_reduce(cnt, out, AX_X, ALU.add))
                link(nc.vector.tensor_scalar(cnt, cnt, -1.0, float(k), ALU.mult, ALU.add))
                link(nc.vector.tensor_tensor_scan(t2.rearrange(flat), resets, t1.rearrange(flat), 0.0,
                                                  ALU.mult, ALU.add))
                link(nc.vector.tensor_tensor(t2, t2, cnt.unsqueeze(2).broadcast_to([P, TT, n]), ALU.is_le))
                link(nc.vector.tensor_tensor(t1, t1, t2, ALU.mult))
                link(nc.vector.tensor_tensor(out, out, t1, ALU.add))

            def choose_groups(p):
                dve.wait_ge(tanh_done, p + 1)
                if p:
                    dve.wait_ge(comb_done, p)
                link(nc.vector.tensor_scalar(score[:], score[:], 0.5, 0.5, ALU.mult, ALU.add))
                link(nc.vector.tensor_tensor(choice[:], score[:], bias.unsqueeze(1).broadcast_to([P, TT, E]),
                                             ALU.add))
                by_two = choice[:].rearrange("p t (g a b) -> p (t g) a b", g=GROUPS, b=2)
                link(nc.vector.tensor_tensor(pair[:, 0], by_two[:, :, :, 0], by_two[:, :, :, 1], ALU.max))
                link(nc.vector.tensor_tensor(pair[:, 1], by_two[:, :, :, 0], by_two[:, :, :, 1], ALU.min))
                flat4 = [g4[:, i].rearrange("p t g -> p (t g)") for i in range(8)]
                link(nc.vector.tensor_tensor(flat4[0], pair[:, 0, :, 0], pair[:, 0, :, 1], ALU.max))
                link(nc.vector.tensor_tensor(flat4[1], pair[:, 0, :, 0], pair[:, 0, :, 1], ALU.min))
                link(nc.vector.tensor_tensor(flat4[2], pair[:, 1, :, 0], pair[:, 1, :, 1], ALU.max))
                link(nc.vector.tensor_tensor(flat4[1], flat4[1], flat4[2], ALU.max))
                link(nc.vector.tensor_tensor(flat4[3], flat4[0], flat4[1], ALU.add))
                gs = g4[:, 3]
                a, b, c, d = (gs[:, :, i] for i in range(GROUPS))
                hi1, lo1, hi2, lo2, thr, cnt = (g1[:, i] for i in range(6))
                link(nc.vector.tensor_tensor(hi1, a, b, ALU.max))
                link(nc.vector.tensor_tensor(lo1, a, b, ALU.min))
                link(nc.vector.tensor_tensor(hi2, c, d, ALU.max))
                link(nc.vector.tensor_tensor(lo2, c, d, ALU.min))
                link(nc.vector.tensor_tensor(lo1, lo1, lo2, ALU.max))
                link(nc.vector.tensor_tensor(hi1, hi1, hi2, ALU.min))
                link(nc.vector.tensor_tensor(thr, hi1, lo1, ALU.max))
                top(gs, thr, TOP_GROUPS, cst[:, C_RSTG:C_RSTG + TT * GROUPS], g4[:, 4], g4[:, 5], g4[:, 6], cnt)

            def choose_experts(p):
                in_group = g4[:, 4].rearrange("p t g -> p (t g)").unsqueeze(2).broadcast_to(
                    [P, TT * GROUPS, E // GROUPS])
                link(nc.vector.tensor_tensor(rt[:, 0].rearrange("p t (g i) -> p (t g) i", g=GROUPS),
                                             choice[:].rearrange("p t (g i) -> p (t g) i", g=GROUPS),
                                             in_group, ALU.mult))
                for tt in range(TT):
                    ins = nc.vector.max(out=top8[:, tt, :], in_=rt[:, 0, tt, :])
                    link(ins)
                top(rt[:, 0], top8[:, :, TOP_K - 1], TOP_K, cst[:, C_RSTE:C_RSTE + TT * E],
                    rt[:, 1], rt[:, 2], rt[:, 3], g1[:, 5])

            def weigh_experts(p):
                cnt = g1[:, 5]
                link(nc.vector.tensor_tensor(rt[:, 4], rt[:, 1], score[:], ALU.mult))
                link(nc.vector.tensor_reduce(cnt, rt[:, 4], AX_X, ALU.add))
                link(nc.vector.tensor_scalar(cnt, cnt, 1e-20, None, ALU.add))
                link(nc.vector.reciprocal(g1[:, 6], cnt))
                link(nc.vector.tensor_tensor(rt[:, 3], rt[:, 4],
                                             g1[:, 6].unsqueeze(2).broadcast_to([P, TT, E]), ALU.mult))
                link(nc.vector.tensor_scalar(rt[:, 4], rt[:, 3], ROUTE_SCALE, None, ALU.mult))
                if p:
                    dve.wait_ge(comb_tr, p)
                link(nc.vector.tensor_copy(comb2[:, :, 0, :], rt[:, 4]))
                nc.vector.tensor_tensor(comb2[:, :, 1, :], rt[:, 4], comb2[:, :, 0, :].bitcast(F32),
                                        ALU.subtract).then_inc(comb_done, 1)

            def tile(s):
                dve.wait_ge(sil_done, s + 1)
                dve.wait_ge(u_done, s + 1)
                if s >= BR:
                    dve.wait_ge(in_lo_done, s - BR + 1)
                b = inter[:, s % BR, :]
                nc.vector.tensor_tensor(b, sil[:, s % BR, :], U[:], ALU.mult).then_inc(up_done, 1)
                if is_expert(s):
                    dve.wait_ge(up_done, s + 1)
                    dve.wait_ge(cb_done, experts_before(s) + 1)
                    nc.vector.tensor_tensor(b, b, CB[:], ALU.mult).then_inc(scaled_done, 1)

            def add_ffn(p):
                dve.wait_ge(down_done, (p + 1) * TILES)
                xh = half_x(p % HALVES)
                nc.vector.scalar_tensor_tensor(out=xh, in0=Y[:], scalar=0.5, in1=xh, op0=ALU.mult,
                                               op1=ALU.add).then_inc(ffn_added, 1)

            def shift(a):
                h4 = ha[:].rearrange("p k (b t) -> p (k b) t", t=SEQ)
                x4 = xx[:].rearrange("p k (b t) -> p (k b) t", t=SEQ)
                dve.wait_ge(ln_h, NORM[f"a{a}"] + 1)
                nc.vector.tensor_tensor(x4[:, :, 1:SEQ], h4[:, :, 0:SEQ - 1], h4[:, :, 1:SEQ],
                                        ALU.subtract).then_inc(xx_done, 1)
                nc.vector.tensor_tensor(x4[:, :, 0:1], h4[:, :, 1:2], h4[:, :, 0:1],
                                        ALU.subtract).then_inc(xx_done, 1)

            def mix(a, m):
                i = len(MIX) * a + m
                dve.wait_ge(xx_done, 2 * (a + 1))
                if i >= 2:
                    dve.wait_ge(xm_hi_done, i - 1)
                    dve.wait_ge(xm_lo_done, i - 1)
                if m == 1 and a:
                    dve.wait_ge(og_hi_done, a)
                    dve.wait_ge(og_lo_done, a)
                for k in range(K):
                    nc.vector.scalar_tensor_tensor(
                        out=xm[:, m % 2, k, :], in0=xx[:, k, :], scalar=par(f"tm_{MIX[m]}", k),
                        in1=ha[:, k, :], op0=ALU.mult, op1=ALU.add).then_inc(xm_done, 1)

            def before_units(a):
                dve.wait_ge(proj_out, K * len(MIX) * (a + 1))
                nc.vector.tensor_scalar(proj["g"][:], proj["g"][:], 0.5, 0.5, ALU.mult,
                                        ALU.add).then_inc(gate_sig, 1)
                for k in range(K):
                    nc.vector.scalar_tensor_tensor(
                        out=xx[:, k, :], in0=proj["r"][:, k, :], scalar=par("time_first", k),
                        in1=proj["k"][:, k, :], op0=ALU.mult, op1=ALU.mult).then_inc(ruk_done, 1)
                dve.wait_ge(ruk_done, K * (a + 1))
                nc.vector.memset(proj["r"][:].rearrange("p k (b t) -> p (k b) t", t=SEQ)[:, :, 0:1],
                                 0.0).then_inc(r_masked, 1)

            def own_value(a):
                for k in range(K):
                    dve.wait_ge(diag_mm, K * a + k + 1)
                    nc.vector.tensor_tensor(ha[:, k, :], A[k][:], proj["v"][:, k, :],
                                            ALU.mult).then_inc(diag_v, 1)

            def add_diag(a, k):
                i = K * a + k
                dve.wait_ge(red_done, UNITS * a + D * (k + 1))
                dve.wait_ge(diag_v, i + 1)
                nc.vector.tensor_tensor(ysb[:, k, :], O[:], ha[:, k, :], ALU.add).then_inc(o_added, 1)
                dve.wait_ge(o_added, i + 1)
                dve.wait_ge(gate_sig, a + 1)
                nc.vector.tensor_tensor(og[:, k, :], ysb[:, k, :], proj["g"][:, k, :],
                                        ALU.mult).then_inc(o_gated, 1)

            def scan(a, n):
                i = UNITS * a + n
                dve.wait_ge(kv_done, i + 1)
                if i >= SR:
                    wait_rs(dve, i - SR)
                nc.vector.tensor_tensor_scan(state[:, i % SR, 1:N + 1], decay_t[:, n // D, :], kv[:, i % 2, :],
                                             0.0, ALU.mult, ALU.add).then_inc(scan_done, 1)

            def outer(a, n):
                i = UNITS * a + n
                dve.wait_ge(vb_loaded[i % VR], 16 * (i // VR + 1))
                if i >= 2:
                    dve.wait_ge(scan_done, i - 1)
                nc.vector.tensor_tensor(kv[:, i % 2, :], proj["k"][:, n // D, :], vb[:, i % VR, :],
                                        ALU.mult).then_inc(kv_done, 1)

            def slot(a, n):
                i = UNITS * a + n - READ_LAG
                if 0 <= n - READ_LAG < UNITS and not on_pool(i):
                    dve.wait_ge(r_masked, a + 1)
                    read_state(dve, i, (n - READ_LAG) // D, rs_dve)
                if 0 <= n - SCAN_LAG < UNITS:
                    scan(a, n - SCAN_LAG)
                if n < UNITS:
                    outer(a, n)
                if n == D - 1 + SUM_LAG:
                    add_diag(a, 0)

            def out_scale(a):
                norm_scale(NORM[f"o{a}"], xx[:])
                dve.wait_ge(ln_h, NORM[f"o{a}"] + 1)
                for k in range(K):
                    nc.vector.tensor_scalar(ha[:, k, :], xx[:, k, :], par("ln_w", k), par("ln_b", k),
                                            ALU.mult, ALU.add).then_inc(z_step, 1)
                dve.wait_ge(z_step, K * (a + 1))
                for k in range(K):
                    xk = x[:, k, a * N:(a + 1) * N]
                    nc.vector.tensor_tensor(xk, xk, ha[:, k, :], ALU.add).then_inc(att_added, 1)

            dve.wait_ge(c_loaded, 16)
            dve.wait_ge(decay_done, 1)
            dve.wait_ge(dt_set, 2)
            for k in range(K):
                nc.vector.tensor_scalar(decay_t[:, k, :], decay_t[:, k, :], decay[:, k:k + 1], None,
                                        ALU.mult).then_inc(dt_done, 1)
            ffn_center(0)
            ffn_scale(0)
            for s in range(STEPS):
                p, t = divmod(s, TILES)
                a, slots = p - 1, slots_of(p, t)
                for n in slots[:1]:
                    slot(a, n)
                tile(s)
                for n in slots[1:]:
                    slot(a, n)
                if t == 0 and p:
                    add_ffn(p - 1)
                if p == 0:
                    if t == AT_SPLIT:
                        dve.wait_ge(aw_hi_done, 1)
                        nc.vector.tensor_tensor(aw_lo[:], aw_raw, aw_hi[:].bitcast(F32),
                                                ALU.subtract).then_inc(aw_lo_done, 1)
                    if t == AT_NORM_B:
                        ffn_center(1)
                    if t == AT_NORM_B + 1:
                        ffn_scale(1)
                if p in (1, 2):
                    if t == AT_NORM_A:
                        dve.wait_ge(ffn_added, a + 1)
                        norm_center(NORM[f"a{a}"], half_x(a))
                    if t == AT_NORM_A + 1:
                        if a:
                            dve.wait_ge(att_added, K * a)
                        norm_scale(NORM[f"a{a}"], ha[:])
                        shift(a)
                    if AT_MIX <= t < AT_MIX + 2:
                        for m in (2 * (t - AT_MIX), 2 * (t - AT_MIX) + 1):
                            mix(a, m)
                    if t == AT_PREP - 1:
                        dve.wait_ge(dt_done, K)
                        dve.wait_ge(state0_set, 1)
                        dve.wait_ge(aw_hi_done, 1)
                        dve.wait_ge(aw_lo_done, 1)
                        before_units(a)
                    if t == AT_PREP:
                        own_value(a)
                    if t == AT_OUT - 1:
                        add_diag(a, 1)
                    if t == AT_NORM_O:
                        dve.wait_ge(y_out, K * (a + 1))
                        norm_center(NORM[f"o{a}"], ysb)
                    if t == AT_NORM_O + 1:
                        out_scale(a)
                    if t == AT_NORM_F:
                        ffn_center(p + 1)
                    if t == AT_NORM_F + 1:
                        ffn_scale(p + 1)
                for part, work in enumerate((choose_groups, choose_experts, weigh_experts)):
                    if (q := route_part(s, part)) is not None:
                        work(q)
            add_ffn(PASSES - 1)

        @block.tensor
        def _(pe):
            def three(out, w_h, w_l, m_h, m_l, first, last):
                nc.tensor.matmul(out, w_h, m_h, start=first, stop=False)
                nc.tensor.matmul(out, w_l, m_h, start=False, stop=False)
                return nc.tensor.matmul(out, w_h, m_l, start=False, stop=last)

            def norm_mean(n, src):
                for k in range(K):
                    mm = nc.tensor.matmul(A[0][:], ones_c, src[:, k, :], start=(k == 0), stop=(k == K - 1))
                mm.then_inc(ln_mean, 1)

            def norm_var(n):
                pe.wait_ge(ln_sq, n + 1)
                for k in range(K):
                    mm = nc.tensor.matmul(A[1][:], ones_c, sq[:, k, :], start=(k == 0), stop=(k == K - 1))
                mm.then_inc(ln_var, 1)

            def logits(p):
                pe.wait_ge(ln_h, NORM[f"f{p}"] + 1)
                for tt in range(TT):
                    for k in range(K):
                        mm = nc.tensor.matmul(A[0][:, tt * E:(tt + 1) * E], hf[:, k, tt * P:(tt + 1) * P],
                                              gate_t[:, k, :], start=(k == 0), stop=(k == K - 1))
                mm.then_inc(logits_done, 1)

            def turn_comb(p):
                pe.wait_ge(ln_turned, NORM[f"f{p}"] + 1)
                pe.wait_ge(comb_done, p + 1)
                for tt in range(TT):
                    mm = nc.tensor.transpose(A[1][0:2 * E, tt * P:(tt + 1) * P],
                                             comb2[:, tt].rearrange("p h e -> p (h e)").bitcast(F32), ident)
                mm.then_inc(comb_tr, 1)

            def gate_up(s, gu):
                p = s // TILES
                bank, done, free = ((G, g_done, sil_done), (U, u_done, up_done))[gu]
                pe.wait_ge(w_lo_done, s + 1)
                if s % TILES == 0:
                    pe.wait_ge(h_hi_done, p + 1)
                    pe.wait_ge(h_lo_done, p + 1)
                if s:
                    pe.wait_ge(free, s)
                for k in range(K):
                    at = (gu * K + k) * P
                    mm = three(bank[:], w_hi[:, s % WR, at:at + P], w_lo[:, s % WR, at:at + P],
                               h_hi[:, p % 2, k, :], h_lo[:, p % 2, k, :], k == 0, k == K - 1)
                mm.then_inc(done, 1)

            def spread_comb(s):
                p, t = divmod(s, TILES)
                if t < SHARED_TILES:
                    return
                if t == SHARED_TILES:
                    pe.wait_ge(comb_t_done, p + 1)
                if experts_before(s):
                    pe.wait_ge(scaled_done, experts_before(s))
                nc.tensor.matmul(CB[:], sel_e[:, t - SHARED_TILES, :], comb_t[:, p % 2, :], start=True,
                                 stop=True).then_inc(cb_done, 1)

            def down(s):
                p, t = divmod(s, TILES)
                pe.wait_ge(in_hi_done, s + 1)
                pe.wait_ge(in_lo_done, s + 1)
                if t == 0 and p:
                    pe.wait_ge(ffn_added, p)
                for c in range(K):
                    at = 2 * K * P + c * P
                    mm = three(Y[:, c, :], w_hi[:, s % WR, at:at + P], w_lo[:, s % WR, at:at + P],
                               in_hi[:, s % BR, :], in_lo[:, s % BR, :], t == 0, t == TILES - 1)
                mm.then_inc(down_done, 1)

            def project(a, m):
                i = len(MIX) * a + m
                pe.wait_ge(xm_hi_done, i + 1)
                pe.wait_ge(xm_lo_done, i + 1)
                for c in range(K):
                    if m:
                        pe.wait_ge(proj_out, K * (i - 1) + c + 1)
                    for k in range(K):
                        cols = slice(c * P, (c + 1) * P)
                        mm = three(A[c][:], aw_hi[:, m, k, cols], aw_lo[:, m, k, cols],
                                   xm_hi[:, m % 2, k, :], xm_lo[:, m % 2, k, :], k == 0, k == K - 1)
                    mm.then_inc(proj_mm, 1)

            def diag(a):
                pe.wait_ge(ruk_done, K * (a + 1))
                for k in range(K):
                    pe.wait_ge(proj_out, K * len(MIX) * (a + 1))
                    nc.tensor.matmul(A[k][:], head_ones, xx[:, k, :], start=True, stop=True).then_inc(diag_mm, 1)

            def slot(a, n):
                n -= SUM_LAG
                if not 0 <= n < UNITS:
                    return
                i = UNITS * a + n
                k, j = divmod(n, D)
                wait_rs(pe, i)
                if j == 0 and K * a + k:
                    pe.wait_ge(o_added, K * a + k)
                nc.tensor.matmul(O[:], sum_j[:, j, :], rs[:, i % PR, :], start=(j == 0),
                                 stop=(j == D - 1)).then_inc(red_done, 1)

            def out_project(a):
                pe.wait_ge(og_hi_done, a + 1)
                pe.wait_ge(og_lo_done, a + 1)
                pe.wait_ge(diag_v, K * (a + 1))
                for c in range(K):
                    for k in range(K):
                        cols = slice(c * P, (c + 1) * P)
                        mm = three(A[c][:], aw_hi[:, 4, k, cols], aw_lo[:, 4, k, cols],
                                   og_hi[:, k, :], og_lo[:, k, :], k == 0, k == K - 1)
                    mm.then_inc(wo_mm, 1)

            pe.wait_ge(c_loaded, 16)
            pe.wait_ge(x_loaded[0], 16)
            norm_mean(0, half_x(0))
            norm_var(0)
            logits(0)
            pe.wait_ge(sel_loaded, 16)
            for s in range(STEPS + 1):
                p, t = divmod(s, TILES)
                a, slots = p - 1, slots_of(p, t)
                if s < STEPS:
                    gate_up(s, 0)
                    for n in slots[:1]:
                        slot(a, n)
                    gate_up(s, 1)
                    if (q := route_part(s, 3)) is not None:
                        turn_comb(q)
                    spread_comb(s)
                for n in slots[1:2]:
                    slot(a, n)
                if s:
                    down(s - 1)
                for n in slots[2:]:
                    slot(a, n)
                if s == STEPS:
                    break
                if p == 0:
                    if t == AT_NORM_B:
                        pe.wait_ge(x_loaded[1], 16)
                        pe.wait_ge(tanh_done, 1)
                        norm_mean(NORM["f1"], half_x(1))
                    if t == AT_NORM_B + 1:
                        pe.wait_ge(comb_t_done, 1)
                        norm_var(NORM["f1"])
                if p in (1, 2):
                    if t == AT_NORM_A:
                        pe.wait_ge(ffn_added, a + 1)
                        pe.wait_ge(tanh_done, p + 1)
                        norm_mean(NORM[f"a{a}"], half_x(a))
                    if t == AT_NORM_A + 1:
                        pe.wait_ge(comb_t_done, p + 1)
                        norm_var(NORM[f"a{a}"])
                    if AT_MIX < t <= AT_MIX + 2:
                        if t == AT_MIX + 1:
                            pe.wait_ge(ln_turned, NORM[f"a{a}"] + 1)
                            pe.wait_ge(aw_lo_done, 1)
                        for m in (2 * (t - AT_MIX) - 2, 2 * (t - AT_MIX) - 1):
                            project(a, m)
                    if t == AT_PREP:
                        pe.wait_ge(sum_loaded, 16)
                        diag(a)
                    if t == AT_OUT:
                        out_project(a)
                    if t == AT_NORM_O:
                        pe.wait_ge(y_out, K * (a + 1))
                        norm_mean(NORM[f"o{a}"], ysb)
                    if t == AT_NORM_O + 1:
                        norm_var(NORM[f"o{a}"])
                    if t == AT_NORM_F:
                        pe.wait_ge(att_added, K * (a + 1))
                        norm_mean(NORM[f"f{p + 1}"], half_x((p + 1) % HALVES))
                    if t == AT_NORM_F + 1:
                        pe.wait_ge(ln_turned, NORM[f"o{a}"] + 1)
                        norm_var(NORM[f"f{p + 1}"])
                if s and (q := route_part(s, 0)) is not None:
                    logits(q)


def constants():
    c = np.zeros((P, C_END), np.float32)
    c[:, C_ONES:C_ONES + P] = 1.0 / C
    head = np.arange(P) // D
    c[:, C_HEAD:C_HEAD + P] = head[:, None] == head[None, :]
    c[:, C_IDENT:C_IDENT + P] = np.eye(P)
    sums = np.zeros((P, D, P), np.float32)
    for j in range(D):
        sums[:, j, :] = (head[:, None] == head[None, :]) & (np.arange(P) % D == j)[None, :]
    c[:, C_RSTE:C_RSTE + TT * E] = np.arange(TT * E) % E != 0
    c[:, C_RSTG:C_RSTG + TT * GROUPS] = np.arange(TT * GROUPS) % GROUPS != 0
    unit_expert = np.arange(E * I) // I
    exp = (np.arange(2 * E) % E)[:, None] == unit_expert[None, :]
    return c, sums, exp.astype(np.float32).reshape(2 * E, EXPERT_TILES, P)


def kernel(**inputs):
    import concourse.bacc as bacc
    from concourse.bass_utils import run_bass_kernel_spmd

    a = {n.removeprefix("L0_"): np.asarray(v) for n, v in inputs.items()}

    x = np.ascontiguousarray(a["attn_x"].reshape(TOKENS, K, P).transpose(2, 1, 0))

    pad = np.zeros((SHARED_TILES * P - I * N_SHARED, C), np.float32)

    def rows(shared, routed):
        return np.concatenate([shared, pad, routed.reshape(E * I, C)])

    gate = rows(a["ffn_shared_gate_w"], a["ffn_gate_proj"]).reshape(TILES, P, K, P).transpose(0, 3, 2, 1)
    up = rows(a["ffn_shared_up_w"], a["ffn_up_proj"]).reshape(TILES, P, K, P).transpose(0, 3, 2, 1)
    down = rows(a["ffn_shared_down_w"].T, a["ffn_down_proj"].transpose(0, 2, 1)).reshape(TILES, P, C)
    w = np.concatenate([gate.reshape(TILES, P, K * P), up.reshape(TILES, P, K * P), down], axis=2)

    aw = np.stack([a[f"attn_W{m}"].T.reshape(K, P, C).transpose(1, 0, 2) for m in (*MIX, "o")], axis=1)

    c, sums, exp = constants()
    c[:, C_GATE:C_GATE + K * E] = a["ffn_gate_weight"].T.reshape(K, P, E).transpose(1, 0, 2).reshape(P, K * E)
    c[:, C_BIAS:C_BIAS + E] = a["ffn_e_score_correction_bias"]
    for n, name in enumerate(PARAMS):
        c[:, C_PAR + K * n:C_PAR + K * (n + 1)] = a[f"attn_{name}"].reshape(K, P).T

    nc = bacc.Bacc("TRN2", target_bir_lowering=False, num_devices=1)
    arrays, args = {}, []
    for name, v in (("x", x), ("w", w), ("aw", aw), ("consts", c), ("sums", sums), ("exp", exp)):
        v = np.ascontiguousarray(v)
        arrays[f"in_{name}_dram"] = v
        args.append(nc.dram_tensor(f"in_{name}_dram", v.shape, mybir.dt.from_np(v.dtype), kind="ExternalInput").ap())
    args.append(nc.dram_tensor("out_0_dram", (P, K, TOKENS), F32, kind="ExternalOutput").ap())
    macaron(nc, *args)
    r = run_bass_kernel_spmd(nc, [arrays], core_ids=[0])
    out = r.results[0]["out_0_dram"]
    return np.ascontiguousarray(out.transpose(2, 1, 0)).reshape(BATCH, SEQ, C)
```

```python
from contextlib import ExitStack

import concourse.bass as bass
import numpy as np
from concourse import mybir

F32 = mybir.dt.float32
F32R = mybir.dt.float32r
ALU = mybir.AluOpType
ACT = mybir.ActivationFunctionType
AX_X = mybir.AxisListType.X

P = 128
BATCH, SEQ, C = 4, 256, 256
TOKENS = BATCH * SEQ
HALVES = 2
N = TOKENS // HALVES
HB = BATCH // HALVES
K = C // P
HEADS, D = 16, 16
E, I, GROUPS, TOP_GROUPS, TOP_K, N_SHARED = 16, 176, 4, 2, 6, 2
ROUTE_SCALE = 2.5
EPS = 1e-5
SHARED_TILES = -(-I * N_SHARED // P)
EXPERT_TILES = E * I // P
TILES = SHARED_TILES + EXPERT_TILES
PASSES = 2 * HALVES
STEPS = PASSES * TILES
WCOLS = 2 * K * P + C
TT = N // P
UNITS = K * D

RAW, GR, DR = 3, 3, 6
BR, IR = 3, 4
CR = 3
PR, VR, SR = 3, 4, 3
DOWN_LAG = 3
GU = 2 * K * P

C_HEAD, C_IDENT, C_GATE = 0, P, 2 * P
C_BIAS = C_GATE + K * E
C_RSTE = C_BIAS + E
C_RSTG = C_RSTE + TT * E
C_PAR = C_RSTG + TT * GROUPS
PARAMS = ("time_decay", "time_first", "tm_v", "tm_k", "tm_r", "tm_g", "ln_w", "ln_b")
C_END = C_PAR + K * len(PARAMS)
MIX = ("v", "k", "r", "g")

AT_SPLIT, AT_NORM_B, AT_DECAY = 5, 10, 14
AT_NORM_A, AT_MIX, AT_UNITS, AT_PREP = 2, 4, 7, 8
SLOTS_PER_STEP, SCAN_LAG, READ_LAG, SUM_LAG = 4, 1, 2, 4
SLOTS = UNITS + SUM_LAG
V_AHEAD, CB_AHEAD = 4, 3
AT_OUT = AT_UNITS + -(-SLOTS // SLOTS_PER_STEP)
AT_HALF_OUT = AT_UNITS + (D - 1 + SUM_LAG) // SLOTS_PER_STEP + 1
AT_NORM_O, AT_NORM_F = AT_OUT + 1, AT_OUT + 4
assert AT_NORM_F + 2 < TILES


EARLY, MIDDLE, LATE = range(3)


def norm_places():
    places = {"f1": ((AT_NORM_B, LATE), (AT_NORM_B + 1, LATE))}
    for a in range(HALVES):
        at = TILES * (a + 1)
        places[f"a{a}"] = ((at + AT_NORM_A, EARLY), (at + AT_NORM_A + 1, MIDDLE))
        places[f"o{a}"] = ((at + AT_NORM_O, LATE), (at + AT_NORM_O + 1, LATE))
        places[f"f{a + 2}"] = ((at + AT_NORM_F, LATE), (at + AT_NORM_F + 1, LATE))
    return places


PLACES = norm_places()
ROUTE_AT = (-2, AT_NORM_B + 2, TILES + AT_NORM_F + 2, 2 * TILES + AT_NORM_F + 2)


def downs_at(s):
    p, t = divmod(s, TILES)
    if p and t == DOWN_LAG - 2:
        return (s - DOWN_LAG, s - DOWN_LAG + 1)
    if s < DOWN_LAG or p and t == DOWN_LAG - 1:
        return ()
    return (s - DOWN_LAG,)


def means_at(s, *where):
    return [n for n in PLACES if PLACES[n][0][0] == s and PLACES[n][0][1] in where]


def variances_at(s, *where):
    return [n for n in PLACES if PLACES[n][1][0] == s and PLACES[n][1][1] in where]


def turned_at(s, where):
    for q, at in enumerate(ROUTE_AT):
        if (s, where) == (at + 4, MIDDLE if q else EARLY):
            return q
    return None


def routed_at(s):
    return ROUTE_AT.index(s) if s in ROUTE_AT else None


NORM = {"f0": 0, "f1": 1, "a0": 2, "o0": 3, "f2": 4, "a1": 5, "o1": 6, "f3": 7}


def macaron(nc, x_d, w_d, aw_d, c_d, sums_d, comb_d, out_d):
    ctx = ExitStack()
    with ctx:
        def sb(name, shape, dt=F32):
            return ctx.enter_context(nc.sbuf_tensor(name, shape, dt))

        def pb(name, shape):
            return ctx.enter_context(nc.psum_tensor(name, shape, F32))

        def sem(name):
            return ctx.enter_context(nc.semaphore(name))

        cst = sb("cst", [P, C_END])
        ones_c = sb("ones_c", [P, P])
        sum_j = sb("sum_j", [P, D, P])
        head_ones = cst[:, C_HEAD:C_HEAD + P]
        ident = cst[:, C_IDENT:C_IDENT + P]
        gate_t = cst[:, C_GATE:C_GATE + K * E].rearrange("p (k e) -> p k e", k=K)
        bias = cst[:, C_BIAS:C_BIAS + E]

        def par(name, k):
            at = C_PAR + K * PARAMS.index(name) + k
            return cst[:, at:at + 1]

        eps = sb("eps", [P, 1])
        lam = sb("lam", [P, K])
        decay = sb("decay", [P, K])
        decay_t = sb("decay_t", [P, K, N])
        early = sb("early", [P, (2 + PR) * N])
        assert (2 + PR) * N == 5 * K * C
        aw_raw = early[:].rearrange("p (m k c) -> p m k c", m=5, k=K)
        aw_hi = sb("aw_hi", [P, 5, K, C], F32R)
        aw_lo = sb("aw_lo", [P, 5, K, C], F32R)
        x = sb("x", [P, K, TOKENS])
        w_raw = sb("w_raw", [P, RAW, WCOLS])
        w_hi = sb("w_hi", [P, GR, GU], F32R)
        w_lo = sb("w_lo", [P, GR, GU], F32R)
        d_hi = sb("d_hi", [P, DR, C], F32R)
        d_lo = sb("d_lo", [P, DR, C], F32R)
        h_hi = sb("h_hi", [P, 2, K, N], F32R)
        h_lo = sb("h_lo", [P, 2, K, N], F32R)
        sil = sb("sil", [P, BR, N])
        inter = sb("inter", [P, BR, N])
        in_hi = sb("in_hi", [P, IR, N], F32R)
        in_lo = sb("in_lo", [P, IR, N], F32R)
        cb = sb("cb", [P, CR, N])
        var_t = sb("var_t", [P, N // 32, 32])
        sd = sb("sd", [P, N // 32])
        rsd = sb("rsd", [P, N // 32])
        rstd = sb("rstd", [P, N])
        score = sb("score", [P, TT, E])
        choice = sb("choice", [P, TT, E])
        pair = sb("pair", [P, 2, TT * GROUPS, 2])
        g4 = sb("g4", [P, 8, TT, GROUPS])
        g1 = sb("g1", [P, 8, TT])
        rt = sb("rt", [P, 5, TT, E])
        top8 = sb("top8", [P, TT, 8])
        comb = sb("comb", [P, TT, E])
        comb_t = sb("comb_t", [E, N])
        ha = sb("ha", [P, K, N])
        hf = ha
        xx = sb("xx", [P, K, N])
        xm = sb("xm", [P, 2, K, N])
        xc, sq = xm[:, 0], xm[:, 1]
        xm_hi = sb("xm_hi", [P, 2, K, N], F32R)
        xm_lo = sb("xm_lo", [P, 2, K, N], F32R)
        proj = {m: sb(f"{m}_t", [P, K, N]) for m in MIX}
        vb = sb("vb", [P, VR, N])
        kv = early[:, 0:2 * N].rearrange("p (r t) -> p r t", r=2)
        state = sb("state", [P, SR, N + 1])
        rs = early[:, 2 * N:].rearrange("p (r t) -> p r t", r=PR)
        og, og_hi, og_lo = xm[:, 1], xm_hi[:, 1], xm_lo[:, 1]
        ysb = xm[:, 0]

        Y = pb("Y", [P, K, N])
        G = [pb("G0", [P, N]), pb("G1", [P, N])]
        U = [pb("U0", [P, N]), pb("U1", [P, N])]
        A = [pb("A0", [P, N]), pb("A1", [P, N])]

        c_loaded, aw_loaded = sem("c_loaded"), sem("aw_loaded")
        cb_loaded = [sem(f"cb_loaded{i}") for i in range(CR)]
        comb_stored = sem("comb_stored")
        sum_loaded = sem("sum_loaded")
        x_loaded = [sem(f"x_loaded{half}") for half in range(HALVES)]
        w_loaded = [sem(f"w_loaded{i}") for i in range(RAW)]
        ones_set, eps_set, lam_done, decay_done, dt_set, dt_done = (
            sem(n) for n in ("ones_set", "eps_set", "lam_done", "decay_done", "dt_set", "dt_done"))
        state0_set = sem("state0_set")
        aw_hi_done, aw_lo_done = sem("aw_hi_done"), sem("aw_lo_done")
        ln_sum, ln_mean, ln_xc, ln_sq, ln_sqsum, ln_var, ln_turned, ln_sd, ln_rsd, ln_rstd, ln_h = (
            sem(n) for n in ("ln_sum", "ln_mean", "ln_xc", "ln_sq", "ln_sqsum", "ln_var", "ln_turned",
                             "ln_sd", "ln_rsd", "ln_rstd", "ln_h"))
        h_hi_done, h_lo_done = sem("h_hi_done"), sem("h_lo_done")
        w_hi_done, w_lo_done, d_hi_done, d_lo_done = (
            sem(n) for n in ("w_hi_done", "w_lo_done", "d_hi_done", "d_lo_done"))
        g_done, u_done, down_done = sem("g_done"), sem("u_done"), sem("down_done")
        sil_done, up_done, scaled_done = sem("sil_done"), sem("up_done"), sem("scaled_done")
        in_hi_done, in_lo_done, ffn_added = sem("in_hi_done"), sem("in_lo_done"), sem("ffn_added")
        logits_done, tanh_done, route_step, comb_done, comb_tr, comb_t_done = (
            sem(n) for n in ("logits_done", "tanh_done", "route_step", "comb_done", "comb_tr", "comb_t_done"))
        xx_done, xm_done, xm_hi_done, xm_lo_done, proj_mm, proj_out = (
            sem(n) for n in ("xx_done", "xm_done", "xm_hi_done", "xm_lo_done", "proj_mm", "proj_out"))
        gate_sig, ruk_done, r_masked, diag_mm, diag_v = (
            sem(n) for n in ("gate_sig", "ruk_done", "r_masked", "diag_mm", "diag_v"))
        vb_loaded = [sem(f"vb_loaded{i}") for i in range(VR)]
        kv_done, scan_done, rs_done, red_done, o_added, o_gated = (
            sem(n) for n in ("kv_done", "scan_done", "rs_done", "red_done", "o_added", "o_gated"))
        og_hi_done, wo_mm, y_out, z_step, att_added = (
            sem(n) for n in ("og_hi_done", "wo_mm", "y_out", "z_step", "att_added"))
        og_lo_done = [sem(f"og_lo_done{k}") for k in range(K)]
        out_stored = sem("out_stored")

        block = ctx.enter_context(nc.Block())

        def half_x(half):
            return x[:, :, half * N:(half + 1) * N]

        cb_count = {x: ((x % TILES - SHARED_TILES + 1) * P - 1) // I - (x % TILES - SHARED_TILES) * P // I + 1
                    for x in range(STEPS) if x % TILES >= SHARED_TILES}

        def cb_value(s):
            slot = experts_before(s) % CR
            return 16 * sum(c for x, c in cb_count.items() if x <= s and experts_before(x) % CR == slot)

        def over_k(ap):
            return ap.unsqueeze(1).broadcast_to([P, K, N])

        def experts_before(s):
            return s // TILES * EXPERT_TILES + max(0, s % TILES - SHARED_TILES)

        def is_expert(s):
            return s % TILES >= SHARED_TILES

        def slots_of(p, t):
            if p not in (1, 2) or not AT_UNITS <= t < AT_OUT:
                return ()
            first = (t - AT_UNITS) * SLOTS_PER_STEP
            return tuple(n for n in range(first, first + SLOTS_PER_STEP) if n < SLOTS)

        @block.sync
        def _(sp):
            sp.dma_start(half_x(0), x_d[:, :, 0:N]).then_inc(x_loaded[0], 16)

            def load_vb(a, n):
                i = UNITS * a + n
                if n >= UNITS:
                    return
                k, j = divmod(n, D)
                if i >= VR:
                    sp.wait_ge(kv_done, i - VR + 1)
                rows = proj["v"][j::D, k, :]
                sp.dma_start(vb[:, i % VR, :], rows.unsqueeze(1).broadcast_to([P // D, D, N])).then_inc(
                    vb_loaded[i % VR], 16)

            def pieces(s):
                first = (s % TILES - SHARED_TILES) * P
                at = first
                while at < first + P:
                    e = at // I
                    end = min((e + 1) * I, first + P)
                    yield e, at - first, end - first
                    at = end

            def load_cb(s):
                p, t = divmod(s, TILES)
                if s < 0 or not is_expert(s):
                    return
                if t == SHARED_TILES:
                    sp.wait_ge(comb_t_done, p + 1)
                    if p:
                        sp.wait_ge(comb_stored, 16 * p)
                    for x in range(p * TILES - CR, p * TILES):
                        if p:
                            sp.wait_ge(cb_loaded[experts_before(x) % CR], cb_value(x))
                    sp.dma_start(comb_d, comb_t[:]).then_inc(comb_stored, 16)
                    sp.wait_ge(comb_stored, 16 * (p + 1))
                n = experts_before(s)
                if n >= CR:
                    sp.wait_ge(scaled_done, n - CR + 1)
                for e, lo, hi in pieces(s):
                    sp.dma_start(cb[lo:hi, n % CR, :], comb_d[e:e + 1, :].broadcast_to([hi - lo, N])).then_inc(
                        cb_loaded[n % CR], 16)

            for s in range(STEPS + V_AHEAD):
                load_cb(s - CB_AHEAD)
                vp, vt = divmod(s - V_AHEAD, TILES)
                if vp in (1, 2) and vt == AT_UNITS:
                    sp.wait_ge(proj_out, K * (len(MIX) * (vp - 1) + 1))
                    for n in range(VR - 1):
                        load_vb(vp - 1, n)
                for n in slots_of(vp, vt):
                    load_vb(vp - 1, n + VR - 1)
                if s >= STEPS:
                    continue
                if s >= RAW:
                    sp.wait_ge(w_lo_done, s - RAW + 1)
                    sp.wait_ge(d_lo_done, s - RAW + 1)
                sp.dma_start(w_raw[:, s % RAW, :], w_d[s % TILES]).then_inc(w_loaded[s % RAW], 16)
                if s == 1:
                    sp.dma_start(half_x(1), x_d[:, :, N:TOKENS]).then_inc(x_loaded[1], 16)
                if s == 2:
                    sp.dma_start(aw_raw, aw_d).then_inc(aw_loaded, 16)
                if s == 3:
                    sp.dma_start(sum_j[:], sums_d).then_inc(sum_loaded, 16)
            for half in range(HALVES):
                for k in range(K):
                    sp.wait_ge(ffn_added, K * (HALVES + half) + k + 1)
                    sp.dma_start(out_d[:, k, half * N:(half + 1) * N], half_x(half)[:, k, :]).then_inc(out_stored, 16)
            sp.wait_ge(out_stored, 16 * K * HALVES)

        @block.gpsimd
        def _(pool):
            nc.gpsimd.memset(ones_c[:], 1.0 / C).then_inc(ones_set, 1)
            nc.gpsimd.memset(eps[:], EPS).then_inc(eps_set, 1)
            nc.gpsimd.memset(state[:, :, 0:1], 0.0).then_inc(state0_set, 1)
            nc.gpsimd.memset(decay_t[:], 1.0).then_inc(dt_set, 1)
            pool.wait_ge(dt_set, 1)
            starts = decay_t[:].rearrange("p k (b t) -> p (k b) t", t=SEQ)[:, :, 0:1]
            nc.gpsimd.memset(starts, 0.0).then_inc(dt_set, 1)

            def split_w(s):
                pool.wait_ge(w_loaded[s % RAW], 16 * (s // RAW + 1))
                pool.wait_ge(w_hi_done, s + 1)
                if s >= GR:
                    pool.wait_ge(u_done, s - GR + 1)
                nc.gpsimd.tensor_tensor(w_lo[:, s % GR, :], w_raw[:, s % RAW, 0:GU],
                                        w_hi[:, s % GR, :].bitcast(F32), ALU.subtract).then_inc(w_lo_done, 1)

            def scale(s):
                n = experts_before(s)
                pool.wait_ge(sil_done, s + 1)
                pool.wait_ge(cb_loaded[n % CR], cb_value(s))
                nc.gpsimd.tensor_tensor(sil[:, s % BR, :], sil[:, s % BR, :], cb[:, n % CR, :],
                                        ALU.mult).then_inc(scaled_done, 1)

            def slot(a, n):
                n -= READ_LAG
                i = UNITS * a + n
                if 0 <= n < UNITS:
                    pool.wait_ge(r_masked, a + 1)
                    pool.wait_ge(scan_done, i + 1)
                    if i >= PR:
                        pool.wait_ge(red_done, i - PR + 1)
                    nc.gpsimd.tensor_tensor(rs[:, i % PR, :], proj["r"][:, n // D, :], state[:, i % SR, 0:N],
                                            ALU.mult).then_inc(rs_done, 1)

            def og_low(a):
                pool.wait_ge(og_hi_done, K * (a + 1))
                nc.gpsimd.tensor_tensor(og_lo[:, 1, :], og[:, 1, :], og_hi[:, 1, :].bitcast(F32),
                                        ALU.subtract).then_inc(og_lo_done[1], 1)

            split_w(0)
            split_w(1)
            for s in range(STEPS):
                p, t = divmod(s, TILES)
                a, slots = p - 1, slots_of(p, t)
                if is_expert(s):
                    scale(s)
                for n in slots[:2]:
                    slot(a, n)
                if s + 2 < STEPS:
                    split_w(s + 2)
                for n in slots[2:]:
                    slot(a, n)
                if p in (1, 2):
                    if t == AT_OUT - 1:
                        og_low(a)

        @block.scalar
        def _(act):
            act.dma_start(cst[:], c_d).then_inc(c_loaded, 16)

            def set_decay():
                act.wait_ge(c_loaded, 16)
                nc.scalar.activation(lam[:], cst[:, C_PAR:C_PAR + K], ACT.Exp).then_inc(lam_done, 1)
                act.wait_ge(lam_done, 1)
                nc.scalar.activation(decay[:], lam[:], ACT.Exp, scale=-1.0).then_inc(decay_done, 1)

            def norm_squares(n):
                for k in range(K):
                    act.wait_ge(ln_xc, K * n + k + 1)
                    nc.scalar.activation(sq[:, k, :], xc[:, k, :], ACT.Square).then_inc(ln_sq, 1)

            def norm_root(n):
                act.wait_ge(ln_turned, n + 1)
                if n:
                    act.wait_ge(ln_rsd, n)
                else:
                    act.wait_ge(eps_set, 1)
                nc.scalar.activation(sd[:], var_t[:, :, 0], ACT.Sqrt, bias=eps[:, 0:1]).then_inc(ln_sd, 1)

            def h_high(p):
                act.wait_ge(ln_h, NORM[f"f{p}"] + 1)
                if p >= 2:
                    act.wait_ge(u_done, (p - 1) * TILES)
                nc.scalar.copy(h_hi[:, p % 2], hf[:]).then_inc(h_hi_done, 1)

            def route(p):
                act.wait_ge(logits_done, p + 1)
                if p:
                    act.wait_ge(comb_done, p)
                nc.scalar.activation(score[:], A[0][:, 0:TT * E].rearrange("p (t e) -> p t e", t=TT),
                                     ACT.Tanh, scale=0.5).then_inc(tanh_done, 1)

            def route_out(p):
                act.wait_ge(comb_tr, p + 1)
                if p:
                    act.wait_ge(comb_stored, 16 * p)
                nc.scalar.copy(comb_t[:], A[1][0:E, :]).then_inc(comb_t_done, 1)

            def w_high(s):
                act.wait_ge(w_loaded[s % RAW], 16 * (s // RAW + 1))
                if s >= GR:
                    act.wait_ge(u_done, s - GR + 1)
                nc.scalar.copy(w_hi[:, s % GR, :], w_raw[:, s % RAW, 0:GU]).then_inc(w_hi_done, 1)

            def down_high(s):
                act.wait_ge(w_loaded[s % RAW], 16 * (s // RAW + 1))
                if s >= DR:
                    act.wait_ge(down_done, K * (s - DR + 1))
                nc.scalar.copy(d_hi[:, s % DR, :], w_raw[:, s % RAW, GU:WCOLS]).then_inc(d_hi_done, 1)

            def tile(s):
                act.wait_ge(g_done, s + 1)
                if s >= BR:
                    act.wait_ge(up_done, s - BR + 1)
                nc.scalar.activation(sil[:, s % BR, :], G[s % 2][:], ACT.Silu).then_inc(sil_done, 1)

            def tile_high(s):
                act.wait_ge(up_done, s + 1)
                if s >= IR:
                    act.wait_ge(down_done, K * (s - IR + 1))
                nc.scalar.copy(in_hi[:, s % IR, :], inter[:, s % BR, :]).then_inc(in_hi_done, 1)

            def mix_high(a, m):
                i = len(MIX) * a + m
                act.wait_ge(xm_done, 2 * (i + 1))
                if i >= 2:
                    act.wait_ge(proj_mm, K * (i - 1))
                if m < 2 and a:
                    act.wait_ge(wo_mm, K * a)
                nc.scalar.copy(xm_hi[:, m % 2], xm[:, m % 2]).then_inc(xm_hi_done, 1)

            def project_out(a, m):
                for k in range(K):
                    i = K * (len(MIX) * a + m) + k
                    act.wait_ge(proj_mm, i + 1)
                    if a:
                        act.wait_ge(o_gated, K)
                    func = ACT.Tanh if MIX[m] == "g" else ACT.Copy
                    nc.scalar.activation(proj[MIX[m]][:, k, :], A[k][:], func,
                                         scale=0.5 if MIX[m] == "g" else 1.0).then_inc(proj_out, 1)

            def og_high(a, k):
                act.wait_ge(o_gated, K * a + k + 1)
                nc.scalar.copy(og_hi[:, k, :], og[:, k, :]).then_inc(og_hi_done, 1)

            def y_copy(a):
                for k in range(K):
                    act.wait_ge(wo_mm, K * a + k + 1)
                    if a:
                        act.wait_ge(ln_xc, K * (NORM["o0"] + 1))
                    nc.scalar.copy(ysb[:, k, :], A[k][:]).then_inc(y_out, 1)

            set_decay()
            norm_squares(0)
            for s in range(2):
                w_high(s)
                down_high(s)
            norm_root(0)
            h_high(0)
            route(0)
            for s in range(STEPS):
                p, t = divmod(s, TILES)
                a = p - 1
                tile(s)
                if s:
                    tile_high(s - 1)
                if p in (1, 2) and t in (AT_MIX + 2, AT_MIX + 3):
                    project_out(a, 2 * (t - AT_MIX - 2))
                for n in means_at(s, EARLY):
                    norm_squares(NORM[n])
                if s + 2 < STEPS:
                    w_high(s + 2)
                    down_high(s + 2)
                if p in (1, 2) and t == AT_MIX + 2:
                    mix_high(a, 2)
                for n in means_at(s, MIDDLE, LATE):
                    norm_squares(NORM[n])
                for n in variances_at(s, EARLY, MIDDLE, LATE):
                    norm_root(NORM[n])
                    if n[0] == "f":
                        h_high(int(n[1]))
                if p in (1, 2) and t == AT_MIX:
                    mix_high(a, 0)
                    mix_high(a, 1)
                if (q := routed_at(s)) is not None:
                    route(q)
                for where in (EARLY, MIDDLE):
                    if (q := turned_at(s, where)) is not None:
                        route_out(q)
                if p == 0:
                    if 0 <= t - AT_SPLIT < 5:
                        act.wait_ge(aw_loaded, 16)
                        nc.scalar.copy(aw_hi[:, t - AT_SPLIT], aw_raw[:, t - AT_SPLIT]).then_inc(aw_hi_done, 1)
                if p in (1, 2):
                    if t in (AT_MIX + 2, AT_MIX + 3):
                        project_out(a, 2 * (t - AT_MIX - 2) + 1)
                    if t == AT_MIX + 2:
                        mix_high(a, 3)
                    if t == AT_HALF_OUT:
                        og_high(a, 0)
                    if t == AT_OUT - 1:
                        og_high(a, 1)
                    if t == AT_OUT:
                        y_copy(a)
            tile_high(STEPS - 1)

        @block.vector
        def _(dve):
            steps = [0]

            def step(ins):
                steps[0] += 1
                ins.then_inc(route_step, 1)

            def so_far():
                dve.wait_ge(route_step, steps[0])

            def norm_source(name):
                kind, i = name[0], int(name[1])
                if kind == "o":
                    dve.wait_ge(y_out, K * (i + 1))
                    return ysb
                if kind == "a":
                    dve.wait_ge(ffn_added, K * (i + 1))
                elif i < 2:
                    dve.wait_ge(x_loaded[i], 16)
                else:
                    dve.wait_ge(att_added, K * (i - 1))
                return half_x(i % HALVES)

            def norm_sum(name):
                n, src = NORM[name], norm_source(name)
                if n:
                    dve.wait_ge(ln_var, n)
                nc.vector.tensor_tensor(sq[:, 0, :], src[:, 0, :], src[:, 1, :], ALU.add).then_inc(ln_sum, 1)

            def norm_center(name):
                n, src = NORM[name], norm_source(name)
                dve.wait_ge(ln_mean, n + 1)
                if n:
                    dve.wait_ge(ln_sq, K * n)
                    dve.wait_ge(ln_h, n)
                for k in range(K):
                    nc.vector.tensor_tensor(xc[:, k, :], src[:, k, :], A[0][:],
                                            ALU.subtract).then_inc(ln_xc, 1)

            def norm_square_sum(name):
                n = NORM[name]
                dve.wait_ge(ln_sq, K * (n + 1))
                nc.vector.tensor_tensor(sq[:, 0, :], sq[:, 0, :], sq[:, 1, :], ALU.add).then_inc(ln_sqsum, 1)

            def norm_turn(name):
                n = NORM[name]
                dve.wait_ge(ln_var, n + 1)
                if n:
                    dve.wait_ge(ln_sd, n)
                nc.vector.transpose(var_t[:].rearrange("p a b -> p (a b)"), A[1][:]).then_inc(ln_turned, 1)

            def norm_scale(name, dst):
                n = NORM[name]
                dve.wait_ge(ln_sd, n + 1)
                if n:
                    dve.wait_ge(ln_rstd, n)
                nc.vector.reciprocal(rsd[:], sd[:]).then_inc(ln_rsd, 1)
                dve.wait_ge(ln_rsd, n + 1)
                if n:
                    dve.wait_ge(ln_h, n)
                nc.vector.transpose(rstd[:].rearrange("p (a b) -> p a b", b=32),
                                    rsd[:].unsqueeze(2).broadcast_to([P, N // 32, 32])).then_inc(ln_rstd, 1)
                dve.wait_ge(ln_rstd, n + 1)
                dve.wait_ge(ln_xc, K * (n + 1))
                nc.vector.tensor_tensor(dst, xc, over_k(rstd[:]), ALU.mult).then_inc(ln_h, 1)

            def ffn_scale(p):
                if p:
                    dve.wait_ge(logits_done, p)
                    dve.wait_ge(h_hi_done, p)
                    dve.wait_ge(h_lo_done, p)
                norm_scale(f"f{p}", hf[:])

            def ffn_low(p):
                dve.wait_ge(h_hi_done, p + 1)
                if p >= 2:
                    dve.wait_ge(u_done, (p - 1) * TILES)
                nc.vector.tensor_tensor(h_lo[:, p % 2], hf[:], h_hi[:, p % 2].bitcast(F32),
                                        ALU.subtract).then_inc(h_lo_done, 1)

            def top(values, thr, k, resets, out, t1, t2, cnt):
                n = values.shape[2]
                wide = thr.unsqueeze(2).broadcast_to([P, TT, n])
                flat = "p t n -> p (t n)"
                step(nc.vector.tensor_tensor(out, values, wide, ALU.is_gt))
                step(nc.vector.tensor_tensor(t1, values, wide, ALU.is_equal))
                so_far()
                step(nc.vector.tensor_reduce(cnt, out, AX_X, ALU.add))
                step(nc.vector.tensor_tensor_scan(t2.rearrange(flat), resets, t1.rearrange(flat), 0.0,
                                                  ALU.mult, ALU.add))
                so_far()
                step(nc.vector.tensor_tensor(t2, t2, cnt.unsqueeze(2).broadcast_to([P, TT, n]), ALU.add))
                so_far()
                step(nc.vector.scalar_tensor_tensor(out=t1.rearrange(flat), in0=t2.rearrange(flat),
                                                    scalar=float(k), in1=t1.rearrange(flat),
                                                    op0=ALU.is_le, op1=ALU.mult))
                so_far()
                step(nc.vector.tensor_tensor(out, out, t1, ALU.add))

            by_expert = "p t (g i) -> p (t g) i"

            def choose_groups(p):
                dve.wait_ge(tanh_done, p + 1)
                if p:
                    dve.wait_ge(comb_done, p)
                step(nc.vector.tensor_scalar(score[:], score[:], 0.5, 0.5, ALU.mult, ALU.add))
                so_far()
                step(nc.vector.tensor_tensor(choice[:], score[:], bias.unsqueeze(1).broadcast_to([P, TT, E]),
                                             ALU.add))
                so_far()
                by_two = choice[:].rearrange("p t (g a b) -> p (t g) a b", g=GROUPS, b=2)
                step(nc.vector.tensor_tensor(pair[:, 0], by_two[:, :, :, 0], by_two[:, :, :, 1], ALU.max))
                step(nc.vector.tensor_tensor(pair[:, 1], by_two[:, :, :, 0], by_two[:, :, :, 1], ALU.min))
                so_far()
                flat4 = [g4[:, i].rearrange("p t g -> p (t g)") for i in range(8)]
                step(nc.vector.tensor_tensor(flat4[0], pair[:, 0, :, 0], pair[:, 0, :, 1], ALU.max))
                step(nc.vector.tensor_tensor(flat4[1], pair[:, 0, :, 0], pair[:, 0, :, 1], ALU.min))
                step(nc.vector.tensor_tensor(flat4[2], pair[:, 1, :, 0], pair[:, 1, :, 1], ALU.max))
                so_far()
                step(nc.vector.tensor_tensor(flat4[7], flat4[1], flat4[2], ALU.max))
                so_far()
                step(nc.vector.tensor_tensor(flat4[3], flat4[0], flat4[7], ALU.add))
                so_far()
                gs = g4[:, 3]
                a, b, c, d = (gs[:, :, i] for i in range(GROUPS))
                hi1, lo1, hi2, lo2, thr, cnt, hi, lo = (g1[:, i] for i in range(8))
                step(nc.vector.tensor_tensor(hi1, a, b, ALU.max))
                step(nc.vector.tensor_tensor(lo1, a, b, ALU.min))
                step(nc.vector.tensor_tensor(hi2, c, d, ALU.max))
                step(nc.vector.tensor_tensor(lo2, c, d, ALU.min))
                so_far()
                step(nc.vector.tensor_tensor(lo, lo1, lo2, ALU.max))
                step(nc.vector.tensor_tensor(hi, hi1, hi2, ALU.min))
                so_far()
                step(nc.vector.tensor_tensor(thr, hi, lo, ALU.max))
                so_far()

            def choose_experts(p):
                gs = g4[:, 3]
                top(gs, g1[:, 4], TOP_GROUPS, cst[:, C_RSTG:C_RSTG + TT * GROUPS], g4[:, 4], g4[:, 5],
                    g4[:, 6], g1[:, 5])
                so_far()
                in_group = g4[:, 4].rearrange("p t g -> p (t g)").unsqueeze(2).broadcast_to(
                    [P, TT * GROUPS, E // GROUPS])
                step(nc.vector.tensor_tensor(rt[:, 0].rearrange(by_expert, g=GROUPS),
                                             choice[:].rearrange(by_expert, g=GROUPS), in_group, ALU.mult))
                so_far()
                for tt in range(TT):
                    step(nc.vector.max(out=top8[:, tt, :], in_=rt[:, 0, tt, :]))
                so_far()

            def weigh_experts(p):
                top(rt[:, 0], top8[:, :, TOP_K - 1], TOP_K, cst[:, C_RSTE:C_RSTE + TT * E],
                    rt[:, 1], rt[:, 2], rt[:, 3], g1[:, 5])
                so_far()
                total, scale = g1[:, 5], g1[:, 6]
                step(nc.vector.tensor_tensor(rt[:, 4], rt[:, 1], score[:], ALU.mult))
                so_far()
                step(nc.vector.tensor_reduce(total, rt[:, 4], AX_X, ALU.add))
                so_far()
                step(nc.vector.tensor_scalar(total, total, 1e-20, None, ALU.add))
                so_far()
                step(nc.vector.reciprocal(scale, total))
                so_far()
                step(nc.vector.tensor_tensor(rt[:, 3], rt[:, 4], scale.unsqueeze(2).broadcast_to([P, TT, E]),
                                             ALU.mult))
                so_far()
                if p:
                    dve.wait_ge(comb_tr, p)
                nc.vector.tensor_scalar(comb[:], rt[:, 3], ROUTE_SCALE, None, ALU.mult).then_inc(comb_done, 1)

            def tile(s):
                if is_expert(s):
                    dve.wait_ge(scaled_done, experts_before(s) + 1)
                else:
                    dve.wait_ge(sil_done, s + 1)
                dve.wait_ge(u_done, s + 1)
                if s >= BR:
                    dve.wait_ge(in_lo_done, s - BR + 1)
                nc.vector.tensor_tensor(inter[:, s % BR, :], sil[:, s % BR, :], U[s % 2][:], ALU.mult).then_inc(up_done, 1)

            def down_low(s):
                dve.wait_ge(d_hi_done, s + 1)
                if s >= DR:
                    dve.wait_ge(down_done, K * (s - DR + 1))
                nc.vector.tensor_tensor(d_lo[:, s % DR, :], w_raw[:, s % RAW, GU:WCOLS],
                                        d_hi[:, s % DR, :].bitcast(F32), ALU.subtract).then_inc(d_lo_done, 1)

            def tile_low(s):
                dve.wait_ge(in_hi_done, s + 1)
                if s >= IR:
                    dve.wait_ge(down_done, K * (s - IR + 1))
                nc.vector.tensor_tensor(in_lo[:, s % IR, :], inter[:, s % BR, :],
                                        in_hi[:, s % IR, :].bitcast(F32), ALU.subtract).then_inc(in_lo_done, 1)

            def add_ffn(p):
                for k in range(K):
                    dve.wait_ge(down_done, K * ((p + 1) * TILES - 1) + k + 1)
                    xk = half_x(p % HALVES)[:, k, :]
                    nc.vector.scalar_tensor_tensor(out=xk, in0=Y[:, k, :], scalar=0.5, in1=xk, op0=ALU.mult,
                                                   op1=ALU.add).then_inc(ffn_added, 1)

            def shift(a):
                h4 = ha[:].rearrange("p k (b t) -> p (k b) t", t=SEQ)
                x4 = xx[:].rearrange("p k (b t) -> p (k b) t", t=SEQ)
                dve.wait_ge(ln_h, NORM[f"a{a}"] + 1)
                nc.vector.tensor_tensor(x4[:, :, 1:SEQ], h4[:, :, 0:SEQ - 1], h4[:, :, 1:SEQ],
                                        ALU.subtract).then_inc(xx_done, 1)
                nc.vector.tensor_tensor(x4[:, :, 0:1], h4[:, :, 1:2], h4[:, :, 0:1],
                                        ALU.subtract).then_inc(xx_done, 1)

            def mix(a, m):
                i = len(MIX) * a + m
                dve.wait_ge(xx_done, 2 * (a + 1))
                if i >= 2:
                    dve.wait_ge(xm_hi_done, i - 1)
                    dve.wait_ge(xm_lo_done, i - 1)
                if m == 1 and a:
                    dve.wait_ge(og_hi_done, K * a)
                    for k in range(K):
                        dve.wait_ge(og_lo_done[k], a)
                for k in range(K):
                    nc.vector.scalar_tensor_tensor(
                        out=xm[:, m % 2, k, :], in0=xx[:, k, :], scalar=par(f"tm_{MIX[m]}", k),
                        in1=ha[:, k, :], op0=ALU.mult, op1=ALU.add).then_inc(xm_done, 1)

            def gate(a):
                dve.wait_ge(proj_out, K * len(MIX) * (a + 1))
                nc.vector.tensor_scalar(proj["g"][:], proj["g"][:], 0.5, 0.5, ALU.mult,
                                        ALU.add).then_inc(gate_sig, 1)

            def mix_low(a, m):
                i = len(MIX) * a + m
                dve.wait_ge(xm_hi_done, i + 1)
                if i >= 2:
                    dve.wait_ge(proj_mm, K * (i - 1))
                if m < 2 and a:
                    dve.wait_ge(wo_mm, K * a)
                nc.vector.tensor_tensor(xm_lo[:, m % 2], xm[:, m % 2], xm_hi[:, m % 2].bitcast(F32),
                                        ALU.subtract).then_inc(xm_lo_done, 1)

            def before_units(a):
                dve.wait_ge(proj_out, K * (len(MIX) * a + MIX.index("r") + 1))
                for k in range(K):
                    nc.vector.scalar_tensor_tensor(
                        out=xx[:, k, :], in0=proj["r"][:, k, :], scalar=par("time_first", k),
                        in1=proj["k"][:, k, :], op0=ALU.mult, op1=ALU.mult).then_inc(ruk_done, 1)
                dve.wait_ge(ruk_done, K * (a + 1))
                nc.vector.memset(proj["r"][:].rearrange("p k (b t) -> p (k b) t", t=SEQ)[:, :, 0:1],
                                 0.0).then_inc(r_masked, 1)

            def own_value(a, k):
                dve.wait_ge(diag_mm, K * a + k + 1)
                nc.vector.tensor_tensor(ha[:, k, :], A[1][:], proj["v"][:, k, :], ALU.mult).then_inc(diag_v, 1)

            def add_diag(a, k):
                i = K * a + k
                dve.wait_ge(red_done, UNITS * a + D * (k + 1))
                dve.wait_ge(diag_v, i + 1)
                nc.vector.tensor_tensor(ysb[:, k, :], A[k][:], ha[:, k, :], ALU.add).then_inc(o_added, 1)
                dve.wait_ge(o_added, i + 1)
                dve.wait_ge(gate_sig, a + 1)
                nc.vector.tensor_tensor(og[:, k, :], ysb[:, k, :], proj["g"][:, k, :],
                                        ALU.mult).then_inc(o_gated, 1)

            def og_low(a):
                dve.wait_ge(og_hi_done, K * a + 1)
                nc.vector.tensor_tensor(og_lo[:, 0, :], og[:, 0, :], og_hi[:, 0, :].bitcast(F32),
                                        ALU.subtract).then_inc(og_lo_done[0], 1)

            def scan(a, n):
                i = UNITS * a + n
                dve.wait_ge(kv_done, i + 1)
                if i >= SR:
                    dve.wait_ge(rs_done, i - SR + 1)
                nc.vector.tensor_tensor_scan(state[:, i % SR, 1:N + 1], decay_t[:, n // D, :], kv[:, i % 2, :],
                                             0.0, ALU.mult, ALU.add).then_inc(scan_done, 1)

            def outer(a, n):
                i = UNITS * a + n
                if n == 0:
                    dve.wait_ge(proj_out, K * (len(MIX) * a + MIX.index("k") + 1))
                dve.wait_ge(vb_loaded[i % VR], 16 * (i // VR + 1))
                if i >= 2:
                    dve.wait_ge(scan_done, i - 1)
                nc.vector.tensor_tensor(kv[:, i % 2, :], proj["k"][:, n // D, :], vb[:, i % VR, :],
                                        ALU.mult).then_inc(kv_done, 1)

            def slot(a, n):
                if 0 <= n - SCAN_LAG < UNITS:
                    scan(a, n - SCAN_LAG)
                if n < UNITS:
                    outer(a, n)
                if n == D - 1 + SUM_LAG:
                    add_diag(a, 0)

            def out_scale(a):
                norm_scale(f"o{a}", xx[:])
                dve.wait_ge(ln_h, NORM[f"o{a}"] + 1)
                for k in range(K):
                    nc.vector.tensor_scalar(ha[:, k, :], xx[:, k, :], par("ln_w", k), par("ln_b", k),
                                            ALU.mult, ALU.add).then_inc(z_step, 1)
                dve.wait_ge(z_step, K * (a + 1))
                for k in range(K):
                    xk = x[:, k, a * N:(a + 1) * N]
                    nc.vector.tensor_tensor(xk, xk, ha[:, k, :], ALU.add).then_inc(att_added, 1)

            def units_begin():
                dve.wait_ge(dt_done, K)
                dve.wait_ge(state0_set, 1)
                dve.wait_ge(aw_hi_done, 5)
                dve.wait_ge(aw_lo_done, 5)

            def attention_scale(a):
                if a:
                    dve.wait_ge(att_added, K * a)
                norm_scale(f"a{a}", ha[:])
                shift(a)

            def norms(s, *where):
                for n in means_at(s, *where):
                    norm_center(n)
                for n in variances_at(s, *where):
                    norm_turn(n)
                    i = int(n[1])
                    if n[0] == "f":
                        ffn_scale(i)
                    elif n[0] == "o":
                        out_scale(i)
                        norm_sum(f"f{i + 2}")
                    else:
                        attention_scale(i)

            def spread_decay():
                dve.wait_ge(decay_done, 1)
                dve.wait_ge(dt_set, 2)
                for k in range(K):
                    nc.vector.tensor_scalar(decay_t[:, k, :], decay_t[:, k, :], decay[:, k:k + 1], None,
                                            ALU.mult).then_inc(dt_done, 1)

            norm_sum("f0")
            norm_center("f0")
            norm_square_sum("f0")
            norm_turn("f0")
            ffn_scale(0)
            ffn_low(0)
            down_low(0)
            down_low(1)
            choose_groups(0)
            choose_experts(0)
            weigh_experts(0)
            for s in range(STEPS):
                p, t = divmod(s, TILES)
                a, slots = p - 1, slots_of(p, t)
                if p in (1, 2) and t == AT_UNITS:
                    units_begin()
                for n in slots[:2]:
                    slot(a, n)
                if s:
                    tile_low(s - 1)
                if t == DOWN_LAG - 2 and p:
                    add_ffn(p - 1)
                    if p in (1, 2):
                        norm_sum(f"a{a}")
                for n in means_at(s, EARLY, MIDDLE, LATE):
                    if n[0] == "o":
                        norm_sum(n)
                norms(s, EARLY, MIDDLE)
                if (q := routed_at(s - 1)) is not None:
                    choose_experts(q)
                if p in (1, 2) and t == AT_MIX:
                    mix(a, 0)
                    mix(a, 1)
                    mix_low(a, 0)
                tile(s)
                if p in (1, 2) and t == AT_MIX:
                    mix_low(a, 1)
                if p in (1, 2) and t == AT_UNITS:
                    before_units(a)
                for n in slots[2:]:
                    slot(a, n)
                norms(s, LATE)
                for n in means_at(s, EARLY, MIDDLE, LATE):
                    norm_square_sum(n)
                if s + 2 < STEPS:
                    down_low(s + 2)
                for n in variances_at(s, EARLY, MIDDLE, LATE):
                    if n[0] == "f":
                        ffn_low(int(n[1]))
                if (q := routed_at(s)) is not None:
                    choose_groups(q)
                if s and (q := routed_at(s - 2)) is not None:
                    weigh_experts(q)
                if p == 0:
                    if t == AT_NORM_B - 1:
                        norm_sum("f1")
                    if 0 <= t - AT_SPLIT < 5:
                        m = t - AT_SPLIT
                        dve.wait_ge(aw_hi_done, m + 1)
                        nc.vector.tensor_tensor(aw_lo[:, m], aw_raw[:, m], aw_hi[:, m].bitcast(F32),
                                                ALU.subtract).then_inc(aw_lo_done, 1)
                    if t == AT_DECAY:
                        spread_decay()
                if p in (1, 2):
                    if t == AT_MIX + 1:
                        mix(a, 2)
                        mix(a, 3)
                    if t == AT_MIX + 2:
                        mix_low(a, 2)
                        mix_low(a, 3)
                    if t == AT_PREP:
                        gate(a)
                    if AT_PREP <= t < AT_PREP + K:
                        own_value(a, t - AT_PREP)
                    if t == AT_HALF_OUT + 1:
                        og_low(a)
                    if t == AT_OUT - 1:
                        add_diag(a, 1)
            tile_low(STEPS - 1)
            add_ffn(PASSES - 1)

        @block.tensor
        def _(pe):
            def three(out, w_h, w_l, m_h, m_l, first, last):
                nc.tensor.matmul(out, w_h, m_h, start=first, stop=False)
                nc.tensor.matmul(out, w_l, m_h, start=False, stop=False)
                return nc.tensor.matmul(out, w_h, m_l, start=False, stop=last)

            def norm_mean(name):
                n = NORM[name]
                pe.wait_ge(ln_sum, n + 1)
                if n:
                    pe.wait_ge(ln_xc, K * n)
                nc.tensor.matmul(A[0][:], ones_c[:], sq[:, 0, :], start=True, stop=True).then_inc(ln_mean, 1)

            def norm_var(name):
                n = NORM[name]
                pe.wait_ge(ln_sqsum, n + 1)
                if n:
                    pe.wait_ge(ln_turned, n)
                nc.tensor.matmul(A[1][:], ones_c[:], sq[:, 0, :], start=True, stop=True).then_inc(ln_var, 1)

            def logits(p):
                pe.wait_ge(ln_h, NORM[f"f{p}"] + 1)
                for tt in range(TT):
                    for k in range(K):
                        mm = nc.tensor.matmul(A[0][:, tt * E:(tt + 1) * E], hf[:, k, tt * P:(tt + 1) * P],
                                              gate_t[:, k, :], start=(k == 0), stop=(k == K - 1))
                mm.then_inc(logits_done, 1)

            def turn_comb(p):
                pe.wait_ge(ln_turned, NORM[f"f{p}"] + 1)
                pe.wait_ge(comb_done, p + 1)
                for tt in range(TT):
                    mm = nc.tensor.transpose(A[1][0:E, tt * P:(tt + 1) * P], comb[:, tt], ident)
                mm.then_inc(comb_tr, 1)

            def gate_up(s, gu):
                p = s // TILES
                bank, done, free = ((G, g_done, sil_done), (U, u_done, up_done))[gu]
                pe.wait_ge(w_lo_done, s + 1)
                if s % TILES == 0:
                    pe.wait_ge(h_hi_done, p + 1)
                    pe.wait_ge(h_lo_done, p + 1)
                if s >= 2:
                    pe.wait_ge(free, s - 1)
                for k in range(K):
                    at = (gu * K + k) * P
                    mm = three(bank[s % 2][:], w_hi[:, s % GR, at:at + P], w_lo[:, s % GR, at:at + P],
                               h_hi[:, p % 2, k, :], h_lo[:, p % 2, k, :], k == 0, k == K - 1)
                mm.then_inc(done, 1)

            def down(s):
                p, t = divmod(s, TILES)
                pe.wait_ge(d_lo_done, s + 1)
                pe.wait_ge(in_hi_done, s + 1)
                pe.wait_ge(in_lo_done, s + 1)
                if t == 0 and p:
                    pe.wait_ge(ffn_added, K * p)
                for c in range(K):
                    cols = slice(c * P, (c + 1) * P)
                    mm = three(Y[:, c, :], d_hi[:, s % DR, cols], d_lo[:, s % DR, cols],
                               in_hi[:, s % IR, :], in_lo[:, s % IR, :], t == 0, t == TILES - 1)
                    mm.then_inc(down_done, 1)

            def project(a, m):
                i = len(MIX) * a + m
                pe.wait_ge(xm_hi_done, i + 1)
                pe.wait_ge(xm_lo_done, i + 1)
                pe.wait_ge(aw_lo_done, m + 1)
                for c in range(K):
                    if m == 0:
                        pe.wait_ge(ln_turned, NORM[f"a{a}"] + 1)
                    else:
                        pe.wait_ge(proj_out, K * (i - 1) + c + 1)
                    for k in range(K):
                        cols = slice(c * P, (c + 1) * P)
                        mm = three(A[c][:], aw_hi[:, m, k, cols], aw_lo[:, m, k, cols],
                                   xm_hi[:, m % 2, k, :], xm_lo[:, m % 2, k, :], k == 0, k == K - 1)
                    mm.then_inc(proj_mm, 1)

            def diag(a, k):
                pe.wait_ge(sum_loaded, 16)
                pe.wait_ge(ruk_done, K * a + k + 1)
                pe.wait_ge(proj_out, K * len(MIX) * (a + 1))
                if k:
                    pe.wait_ge(diag_v, K * a + k)
                nc.tensor.matmul(A[1][:], head_ones, xx[:, k, :], start=True, stop=True).then_inc(diag_mm, 1)

            def slot(a, n):
                n -= SUM_LAG
                if not 0 <= n < UNITS:
                    return
                i = UNITS * a + n
                k, j = divmod(n, D)
                pe.wait_ge(rs_done, i + 1)
                if j == 0:
                    pe.wait_ge(sum_loaded, 16)
                    pe.wait_ge(proj_out, K * len(MIX) * (a + 1))
                    if k:
                        pe.wait_ge(diag_v, K * (a + 1))
                nc.tensor.matmul(A[k][:], sum_j[:, j, :], rs[:, i % PR, :], start=(j == 0),
                                 stop=(j == D - 1)).then_inc(red_done, 1)

            def out_project(a):
                pe.wait_ge(diag_v, K * (a + 1))
                for k in range(K):
                    pe.wait_ge(og_hi_done, K * a + k + 1)
                    pe.wait_ge(og_lo_done[k], a + 1)
                    for c in range(K):
                        cols = slice(c * P, (c + 1) * P)
                        if k == 0:
                            pe.wait_ge(o_added, K * a + c + 1)
                        mm = three(A[c][:], aw_hi[:, 4, k, cols], aw_lo[:, 4, k, cols],
                                   og_hi[:, k, :], og_lo[:, k, :], k == 0, k == K - 1)
                        if k == K - 1:
                            mm.then_inc(wo_mm, 1)

            def others(s, where):
                p, t = divmod(s, TILES)
                a = p - 1
                for n in means_at(s, where):
                    if n[0] != "o":
                        pe.wait_ge(tanh_done, p + 1)
                    norm_mean(n)
                for n in variances_at(s, where):
                    if n[0] != "o":
                        pe.wait_ge(comb_t_done, p + 1)
                    norm_var(n)
                if where == LATE and (q := routed_at(s)) is not None:
                    logits(q)
                if (q := turned_at(s, where)) is not None:
                    turn_comb(q)
                if where != EARLY and p in (1, 2) and t in (AT_MIX + 2, AT_MIX + 3):
                    project(a, 2 * (t - AT_MIX - 2) + (where == LATE))
                if where == LATE and p in (1, 2):
                    if AT_PREP <= t < AT_PREP + K:
                        diag(a, t - AT_PREP)
                    if t == AT_OUT:
                        out_project(a)

            pe.wait_ge(ones_set, 1)
            norm_mean("f0")
            norm_var("f0")
            pe.wait_ge(c_loaded, 16)
            logits(0)
            for s in range(STEPS + DOWN_LAG - 1):
                p, t = divmod(s, TILES)
                a, slots = p - 1, slots_of(p, t)
                if s < STEPS:
                    gate_up(s, 0)
                    others(s, EARLY)
                for n in slots[:1]:
                    slot(a, n)
                for d in downs_at(s):
                    down(d)
                if s >= STEPS:
                    continue
                others(s, MIDDLE)
                for n in slots[1:2]:
                    slot(a, n)
                gate_up(s, 1)
                for n in slots[2:]:
                    slot(a, n)
                others(s, LATE)


def constants():
    c = np.zeros((P, C_END), np.float32)
    head = np.arange(P) // D
    c[:, C_HEAD:C_HEAD + P] = head[:, None] == head[None, :]
    c[:, C_IDENT:C_IDENT + P] = np.eye(P)
    sums = np.zeros((P, D, P), np.float32)
    for j in range(D):
        sums[:, j, :] = (head[:, None] == head[None, :]) & (np.arange(P) % D == j)[None, :]
    c[:, C_RSTE:C_RSTE + TT * E] = np.arange(TT * E) % E != 0
    c[:, C_RSTG:C_RSTG + TT * GROUPS] = np.arange(TT * GROUPS) % GROUPS != 0
    return c, sums


def kernel(**inputs):
    import concourse.bacc as bacc
    from concourse.bass_utils import run_bass_kernel_spmd

    a = {n.removeprefix("L0_"): np.asarray(v) for n, v in inputs.items()}

    x = np.ascontiguousarray(a["attn_x"].reshape(TOKENS, K, P).transpose(2, 1, 0))

    pad = np.zeros((SHARED_TILES * P - I * N_SHARED, C), np.float32)

    def rows(shared, routed):
        return np.concatenate([shared, pad, routed.reshape(E * I, C)])

    gate = rows(a["ffn_shared_gate_w"], a["ffn_gate_proj"]).reshape(TILES, P, K, P).transpose(0, 3, 2, 1)
    up = rows(a["ffn_shared_up_w"], a["ffn_up_proj"]).reshape(TILES, P, K, P).transpose(0, 3, 2, 1)
    down = rows(a["ffn_shared_down_w"].T, a["ffn_down_proj"].transpose(0, 2, 1)).reshape(TILES, P, C)
    w = np.concatenate([gate.reshape(TILES, P, K * P), up.reshape(TILES, P, K * P), down], axis=2)

    aw = np.stack([a[f"attn_W{m}"].T.reshape(K, P, C).transpose(1, 0, 2) for m in (*MIX, "o")], axis=1)

    c, sums = constants()
    c[:, C_GATE:C_GATE + K * E] = a["ffn_gate_weight"].T.reshape(K, P, E).transpose(1, 0, 2).reshape(P, K * E)
    c[:, C_BIAS:C_BIAS + E] = a["ffn_e_score_correction_bias"]
    for n, name in enumerate(PARAMS):
        c[:, C_PAR + K * n:C_PAR + K * (n + 1)] = a[f"attn_{name}"].reshape(K, P).T

    nc = bacc.Bacc("TRN2", target_bir_lowering=False, num_devices=1)
    arrays, args = {}, []
    for name, v in (("x", x), ("w", w), ("aw", aw), ("consts", c), ("sums", sums)):
        v = np.ascontiguousarray(v)
        arrays[f"in_{name}_dram"] = v
        args.append(nc.dram_tensor(f"in_{name}_dram", v.shape, mybir.dt.from_np(v.dtype), kind="ExternalInput").ap())
    args.append(nc.dram_tensor("comb_dram", (E, N), F32, kind="Internal").ap())
    args.append(nc.dram_tensor("out_0_dram", (P, K, TOKENS), F32, kind="ExternalOutput").ap())
    macaron(nc, *args)
    r = run_bass_kernel_spmd(nc, [arrays], core_ids=[0])
    out = r.results[0]["out_0_dram"]
    return np.ascontiguousarray(out.transpose(2, 1, 0)).reshape(BATCH, SEQ, C)
```
